# Optimizing a Trainium2 kernel written in Bass

```python
import numpy as np
import jax
import jax.numpy as jnp

def _softmax(x, axis=-1):
    return jax.nn.softmax(x, axis=axis)

def _gelu(x):
    return jax.nn.gelu(x, approximate=True)

def _silu(x):
    return jax.nn.silu(x)

def _sigmoid(x):
    return jax.nn.sigmoid(x)

def _layernorm(x, axis=-1, eps=1e-05):
    m = jnp.mean(x, axis=axis, keepdims=True)
    v = jnp.var(x, axis=axis, keepdims=True)
    return (x - m) / jnp.sqrt(v + eps)

def _scatter_add(tgt, idx, src, axis=0):
    return tgt.at[idx].add(src)

def _segment_sum(src, seg, n):
    return jax.ops.segment_sum(src, seg, n)
kernel_name = 'mk_macaron_d1_jaxref_r8_110c62'

def setup_inputs(seed: int=0):
    np.random.seed(seed)
    _w = jnp.asarray

    def _L0_attn_setup():
        import jax, jax.numpy as jnp
        import numpy as np
        H = 4
        M = 64
        EPS = 1e-05
        CLAMP = 32.0

        def _rope(x):
            B, T, Hh, D = x.shape
            half = D // 2
            inv_freq = 1.0 / 10000.0 ** (jnp.arange(half, dtype=jnp.float32) / half)
            ang = jnp.arange(T, dtype=jnp.float32)[:, None] * inv_freq[None, :]
            cos = jnp.cos(ang)[None, :, None, :]
            sin = jnp.sin(ang)[None, :, None, :]
            x1, x2 = (x[..., :half], x[..., half:])
            return jnp.concatenate([x1 * cos - x2 * sin, x2 * cos + x1 * sin], axis=-1)

        def _forward(hidden_states, Wq, Wk, Wv, Wg, Wo, sk_w1, sk_w2, sk_b2, sv_w1, sv_w2, sv_b2, gnorm_w):
            x = hidden_states
            B, T, D = x.shape
            Dk = D // H
            Dv = D // H
            q = (x @ Wq).reshape(B, T, H, Dk)
            k = (x @ Wk).reshape(B, T, H, Dk)
            v = (x @ Wv).reshape(B, T, H, Dv)
            q = _rope(q)
            k = _rope(k)
            q = q.transpose(0, 2, 1, 3)
            k = k.transpose(0, 2, 1, 3)
            v = v.transpose(0, 2, 1, 3)
            sk = jnp.clip(x @ sk_w1 @ sk_w2 + sk_b2, -CLAMP, CLAMP).reshape(B, T, H, M).transpose(0, 2, 1, 3)
            sv = jnp.clip(x @ sv_w1 @ sv_w2 + sv_b2, -CLAMP, CLAMP).reshape(B, T, H, M).transpose(0, 2, 1, 3)
            scale = Dk ** (-0.5)
            mask = jnp.tril(jnp.ones((T, T), dtype=bool))
            wk = jnp.exp(sk)
            zk = jnp.cumsum(wk, axis=2)
            S = jnp.einsum('bhtd,bhsd->bhts', q, k)
            S = jnp.where(mask, S, 0.0)
            logits = jnp.einsum('bhts,bhsm->bhtm', S, wk) * scale / zk
            p = jax.nn.softmax(logits, axis=-1)
            wv = jnp.exp(sv)
            zv = jnp.cumsum(wv, axis=2)
            A = jnp.einsum('bhtm,bhsm->bhts', p / zv, wv)
            A = jnp.where(mask, A, 0.0)
            o = jnp.einsum('bhts,bhsd->bhtd', A, v)
            o = o.transpose(0, 2, 1, 3)
            g = (x @ Wg).reshape(B, T, H, Dv)
            on = o * jax.lax.rsqrt(jnp.mean(o * o, axis=-1, keepdims=True) + EPS) * gnorm_w
            o = on * g * jax.nn.sigmoid(g)
            return o.reshape(B, T, H * Dv) @ Wo
        key = jax.random.key(seed)
        ks = jax.random.split(key, 10)
        B, T, D = (2, 256, 128)
        low = 16

        def w(k, shape, s=0.02):
            return jax.random.normal(k, shape, dtype=jnp.float32) * s
        return {'hidden_states': jax.random.normal(ks[0], (B, T, D), dtype=jnp.float32), 'Wq': w(ks[1], (D, D)), 'Wk': w(ks[2], (D, D)), 'Wv': w(ks[3], (D, D)), 'Wg': w(ks[4], (D, D)), 'Wo': w(ks[5], (D, D)), 'sk_w1': w(ks[6], (D, low)), 'sk_w2': w(ks[7], (low, H * M)), 'sk_b2': jnp.zeros((H * M,), dtype=jnp.float32), 'sv_w1': w(ks[8], (D, low)), 'sv_w2': w(ks[9], (low, H * M)), 'sv_b2': jnp.zeros((H * M,), dtype=jnp.float32), 'gnorm_w': jnp.ones((D // H,), dtype=jnp.float32)}
    _L0_attn_in = _L0_attn_setup()

    def _L0_ffn_setup():
        import jax, jax.numpy as jnp
        import numpy as np
        B, S, H = (2, 256, 128)
        E_ROUTED = 8
        TOP_K = 2
        I = 256
        key = jax.random.key(seed)
        ks = jax.random.split(key, 9)
        s = 0.02
        return {'x': jax.random.normal(ks[0], (B, S, H), dtype=jnp.float32), 'shared_gate': jax.random.normal(ks[1], (I, H), dtype=jnp.float32) * s, 'shared_up': jax.random.normal(ks[2], (I, H), dtype=jnp.float32) * s, 'shared_down': jax.random.normal(ks[3], (H, I), dtype=jnp.float32) * s, 'gate_w': jax.random.normal(ks[4], (E_ROUTED, H, I), dtype=jnp.float32) * s, 'up_w': jax.random.normal(ks[5], (E_ROUTED, H, I), dtype=jnp.float32) * s, 'down_w': jax.random.normal(ks[6], (E_ROUTED, I, H), dtype=jnp.float32) * s, 'router_w': jax.random.normal(ks[7], (E_ROUTED, H), dtype=jnp.float32) * s, 'routing_bias': jnp.zeros((E_ROUTED,), dtype=jnp.float32)}
    _L0_ffn_in = _L0_ffn_setup()
    _d = {'L0_attn_hidden_states': _L0_attn_in['hidden_states'], 'L0_attn_Wq': _L0_attn_in['Wq'], 'L0_attn_Wk': _L0_attn_in['Wk'], 'L0_attn_Wv': _L0_attn_in['Wv'], 'L0_attn_Wg': _L0_attn_in['Wg'], 'L0_attn_Wo': _L0_attn_in['Wo'], 'L0_attn_sk_w1': _L0_attn_in['sk_w1'], 'L0_attn_sk_w2': _L0_attn_in['sk_w2'], 'L0_attn_sk_b2': _L0_attn_in['sk_b2'], 'L0_attn_sv_w1': _L0_attn_in['sv_w1'], 'L0_attn_sv_w2': _L0_attn_in['sv_w2'], 'L0_attn_sv_b2': _L0_attn_in['sv_b2'], 'L0_attn_gnorm_w': _L0_attn_in['gnorm_w'], 'L0_ffn_shared_gate': _L0_ffn_in['shared_gate'], 'L0_ffn_shared_up': _L0_ffn_in['shared_up'], 'L0_ffn_shared_down': _L0_ffn_in['shared_down'], 'L0_ffn_gate_w': _L0_ffn_in['gate_w'], 'L0_ffn_up_w': _L0_ffn_in['up_w'], 'L0_ffn_down_w': _L0_ffn_in['down_w'], 'L0_ffn_router_w': _L0_ffn_in['router_w'], 'L0_ffn_routing_bias': _L0_ffn_in['routing_bias']}
    _x0 = _d['L0_attn_hidden_states']
    _d['L0_attn_hidden_states'] = jax.random.normal(jax.random.fold_in(jax.random.key(seed), 1), (1, 2048, 128), dtype=_x0.dtype)
    del _x0
    return _d

def reference(L0_attn_hidden_states, L0_attn_Wq, L0_attn_Wk, L0_attn_Wv, L0_attn_Wg, L0_attn_Wo, L0_attn_sk_w1, L0_attn_sk_w2, L0_attn_sk_b2, L0_attn_sv_w1, L0_attn_sv_w2, L0_attn_sv_b2, L0_attn_gnorm_w, L0_ffn_shared_gate, L0_ffn_shared_up, L0_ffn_shared_down, L0_ffn_gate_w, L0_ffn_up_w, L0_ffn_down_w, L0_ffn_router_w, L0_ffn_routing_bias):

    def _L0_attn_ref(hidden_states, Wq, Wk, Wv, Wg, Wo, sk_w1, sk_w2, sk_b2, sv_w1, sv_w2, sv_b2, gnorm_w):
        import jax, jax.numpy as jnp
        import numpy as np
        H = 4
        M = 64
        EPS = 1e-05
        CLAMP = 32.0

        def _rope(x):
            B, T, Hh, D = x.shape
            half = D // 2
            inv_freq = 1.0 / 10000.0 ** (jnp.arange(half, dtype=jnp.float32) / half)
            ang = jnp.arange(T, dtype=jnp.float32)[:, None] * inv_freq[None, :]
            cos = jnp.cos(ang)[None, :, None, :]
            sin = jnp.sin(ang)[None, :, None, :]
            x1, x2 = (x[..., :half], x[..., half:])
            return jnp.concatenate([x1 * cos - x2 * sin, x2 * cos + x1 * sin], axis=-1)

        def _forward(hidden_states, Wq, Wk, Wv, Wg, Wo, sk_w1, sk_w2, sk_b2, sv_w1, sv_w2, sv_b2, gnorm_w):
            x = hidden_states
            B, T, D = x.shape
            Dk = D // H
            Dv = D // H
            q = (x @ Wq).reshape(B, T, H, Dk)
            k = (x @ Wk).reshape(B, T, H, Dk)
            v = (x @ Wv).reshape(B, T, H, Dv)
            q = _rope(q)
            k = _rope(k)
            q = q.transpose(0, 2, 1, 3)
            k = k.transpose(0, 2, 1, 3)
            v = v.transpose(0, 2, 1, 3)
            sk = jnp.clip(x @ sk_w1 @ sk_w2 + sk_b2, -CLAMP, CLAMP).reshape(B, T, H, M).transpose(0, 2, 1, 3)
            sv = jnp.clip(x @ sv_w1 @ sv_w2 + sv_b2, -CLAMP, CLAMP).reshape(B, T, H, M).transpose(0, 2, 1, 3)
            scale = Dk ** (-0.5)
            mask = jnp.tril(jnp.ones((T, T), dtype=bool))
            wk = jnp.exp(sk)
            zk = jnp.cumsum(wk, axis=2)
            S = jnp.einsum('bhtd,bhsd->bhts', q, k)
            S = jnp.where(mask, S, 0.0)
            logits = jnp.einsum('bhts,bhsm->bhtm', S, wk) * scale / zk
            p = jax.nn.softmax(logits, axis=-1)
            wv = jnp.exp(sv)
            zv = jnp.cumsum(wv, axis=2)
            A = jnp.einsum('bhtm,bhsm->bhts', p / zv, wv)
            A = jnp.where(mask, A, 0.0)
            o = jnp.einsum('bhts,bhsd->bhtd', A, v)
            o = o.transpose(0, 2, 1, 3)
            g = (x @ Wg).reshape(B, T, H, Dv)
            on = o * jax.lax.rsqrt(jnp.mean(o * o, axis=-1, keepdims=True) + EPS) * gnorm_w
            o = on * g * jax.nn.sigmoid(g)
            return o.reshape(B, T, H * Dv) @ Wo
        return _forward(hidden_states, Wq, Wk, Wv, Wg, Wo, sk_w1, sk_w2, sk_b2, sv_w1, sv_w2, sv_b2, gnorm_w)

    def _L0_ffn_ref(x, shared_gate, shared_up, shared_down, gate_w, up_w, down_w, router_w, routing_bias):
        import jax, jax.numpy as jnp
        import numpy as np
        B, S, H = (2, 256, 128)
        E_ROUTED = 8
        TOP_K = 2
        I = 256
        b, s, h = x.shape
        shared = jnp.einsum('bsi,hi->bsh', jax.nn.silu(jnp.einsum('bsh,ih->bsi', x, shared_gate)) * jnp.einsum('bsh,ih->bsi', x, shared_up), shared_down)
        logits = jnp.einsum('bsh,eh->bse', x, router_w) + routing_bias
        probs = jax.nn.sigmoid(logits)
        scores, indices = jax.lax.top_k(probs, TOP_K)
        scores = scores / jnp.sum(scores, axis=-1, keepdims=True)
        t = b * s
        xf = x.reshape(t, h)
        idx = indices.reshape(t, TOP_K)
        sc = scores.reshape(t, TOP_K)
        w = jnp.zeros((t, E_ROUTED), dtype=x.dtype)
        w = w.at[jnp.arange(t)[:, None], idx].add(sc)
        g = jax.nn.silu(jnp.einsum('th,ehi->tei', xf, gate_w))
        u = jnp.einsum('th,ehi->tei', xf, up_w)
        combined = jnp.einsum('tei,eih,te->th', g * u, down_w, w)
        return shared + combined.reshape(b, s, h)
    x = L0_attn_hidden_states
    x = x + 0.5 * _L0_ffn_ref(_layernorm(x, axis=-1), L0_ffn_shared_gate, L0_ffn_shared_up, L0_ffn_shared_down, L0_ffn_gate_w, L0_ffn_up_w, L0_ffn_down_w, L0_ffn_router_w, L0_ffn_routing_bias)
    x = x + _L0_attn_ref(_layernorm(x, axis=-1), L0_attn_Wq, L0_attn_Wk, L0_attn_Wv, L0_attn_Wg, L0_attn_Wo, L0_attn_sk_w1, L0_attn_sk_w2, L0_attn_sk_b2, L0_attn_sv_w1, L0_attn_sv_w2, L0_attn_sv_b2, L0_attn_gnorm_w)
    x = x + 0.5 * _L0_ffn_ref(_layernorm(x, axis=-1), L0_ffn_shared_gate, L0_ffn_shared_up, L0_ffn_shared_down, L0_ffn_gate_w, L0_ffn_up_w, L0_ffn_down_w, L0_ffn_router_w, L0_ffn_routing_bias)
    return x

_drawn_inputs = setup_inputs


def setup_inputs(seed=0):
    import zlib

    import numpy as np

    out = dict(_drawn_inputs(seed))
    spreads = {'L0_attn_sk_b2': (0.0, 2.0),
     'L0_attn_sv_b2': (0.0, 2.0),
     'L0_attn_gnorm_w': (1.0, 0.6),
     'L0_ffn_routing_bias': (0.0, 0.8)}
    factors = {'L0_attn_Wq': 51.539,
     'L0_attn_Wk': 40.681,
     'L0_attn_sk_w1': 33.815,
     'L0_attn_sk_w2': 51.552,
     'L0_attn_sv_w1': 8.0,
     'L0_attn_sv_w2': 21.863,
     'L0_ffn_shared_gate': 6.476,
     'L0_ffn_shared_up': 6.16,
     'L0_ffn_shared_down': 6.097,
     'L0_ffn_gate_w': 8.0,
     'L0_ffn_up_w': 8.0,
     'L0_ffn_down_w': 8.0,
     'L0_ffn_router_w': 8.0}
    for name, (base, spread) in spreads.items():
        noise = np.random.default_rng([zlib.crc32(name.encode()), seed]).standard_normal(out[name].shape)
        drawn = base * np.exp(spread * noise) if base else spread * noise
        out[name] = jnp.asarray(drawn.astype(out[name].dtype))
    for name, factor in factors.items():
        out[name] = (out[name] * factor).astype(out[name].dtype)
    return out
```

```python
from contextlib import ExitStack

import numpy as np
import concourse.bass as bass
from concourse import mybir

ALU = mybir.AluOpType
ACT = mybir.ActivationFunctionType
F32 = mybir.dt.float32
F16 = mybir.dt.float16
U32 = mybir.dt.uint32
AX_X = mybir.AxisListType.X

P = 128
T = 2048
D = 128
NC = T // P
GT = 4
NG = NC // GT
GW = GT * P
ER = 8
E = ER + 1
I = 256
IH = I // P
EW = 3 * I
H = 4
DK = D // H
M = 64
LOW = 16
HM = H * M
EPS = 1e-5
CLAMP = 32.0
XS = 64.0
WS = 64.0
HS = 16.0
SPF = NG * E

C_ID = 0
C_TRI = C_ID + P
C_REST = C_TRI + P
C_HEAD = C_REST + P
C_PAIR = C_HEAD + H
C_IOTA = C_PAIR + 2
C_COS = C_IOTA + ER
C_SIN = C_COS + NC * DK // 2
C_END = C_SIN + NC * DK // 2


def constants():
    half = DK // 2
    inv = np.float32(1.0) / np.float32(10000.0) ** (np.arange(half, dtype=np.float32) / np.float32(half))
    angle = np.arange(T, dtype=np.float32)[:, None] * inv.astype(np.float32)[None, :]
    row = np.arange(P)
    out = np.zeros((P, C_END), np.float32)
    out[:, C_ID:C_ID + P] = np.eye(P)
    out[:, C_TRI:C_TRI + P] = row[:, None] <= row[None, :]
    out[:, C_REST:C_REST + P] = row[:, None] > row[None, :]
    out[:, C_HEAD:C_HEAD + H] = row[:, None] // DK == np.arange(H)[None, :]
    out[:, C_PAIR:C_PAIR + 2] = row[:, None] // M == np.arange(2)[None, :]
    out[:, C_IOTA:C_IOTA + ER] = np.arange(ER)[None, :]
    for at, f in ((C_COS, np.cos), (C_SIN, np.sin)):
        table = f(angle).astype(np.float32).reshape(NC, P, half).transpose(1, 0, 2)
        out[:, at:at + NC * half] = table.reshape(P, NC * half)
    return out


def macaron_kernel(nc, x_in, consts, w_ffn, w_router, router_bias, w_qkvg, w_low, w_slots, w_out, gnorm, out):
    x_d = x_in.rearrange("(g c p) d -> g p c d", p=P, c=GT)
    out_d = out.rearrange("(g c p) d -> g p c d", p=P, c=GT)

    with ExitStack() as ctx:
        def sb(name, shape, dt=F32):
            return ctx.enter_context(nc.sbuf_tensor(name, shape, dt))

        def sem(name):
            return ctx.enter_context(nc.semaphore(name))

        x = sb("x", [P, NC, D])
        cst = sb("cst", [P, C_END])
        wf = sb("wf", [P, E, EW])
        wsc = sb("wsc", [P, EW])
        w_hi = sb("w_hi", [P, E, EW], F16)
        w_lo = sb("w_lo", [P, E, EW], F16)
        wr = sb("wr", [P, ER])
        wrs = sb("wrs", [P, ER])
        wr_hi = sb("wr_hi", [P, ER], F16)
        wr_lo = sb("wr_lo", [P, ER], F16)
        rbias = sb("rbias", [P, ER])
        wqkvg = sb("wqkvg", [P, 4 * D])
        wlow = sb("wlow", [P, 2 * LOW])
        wslots = sb("wslots", [2 * LOW + 1, 2 * HM])
        wo = sb("wo", [P, D])
        gn = sb("gn", [P, D])
        stats = sb("stats", [P, NG, GT, 6])
        mv = sb("mv", [P, NG, GT, 2])
        rstd = sb("rstd", [P, NG, GT])
        shift = sb("shift", [P, NG, GT])
        xn = sb("xn", [P, 2, GT, D])
        xt_hi = sb("xt_hi", [P, T], F16)
        xt_lo = sb("xt_lo", [P, T], F16)
        score_z = sb("score_z", [P, NC, ER])
        score = sb("score", [P, NC, ER])
        top = sb("top", [P, NC, 8])
        top_at = sb("top_at", [P, NC, 8], U32)
        top_af = sb("top_af", [P, NC, 2])
        top_sum = sb("top_sum", [P, NC])
        top_inv = sb("top_inv", [P, NC])
        share = sb("share", [P, NC, 2])
        pick = sb("pick", [P, 2, NC, ER])
        wts = sb("wts", [P, NC, E])
        gate_s = sb("gate_s", [P, IH, GW])
        h32 = sb("h32", [P, IH, GW])
        h_hi = sb("h_hi", [P, NG, IH, GW], F16)
        h_lo = sb("h_lo", [P, NG, IH, GW], F16)
        a_st = sb("a_st", [P, NC, 6])
        a_mv = sb("a_mv", [P, NC, 2])
        a_rstd = sb("a_rstd", [P, NC])
        var_e = sb("var_e", [P, NC])
        power = sb("power", [P, NC])
        a_xn = sb("a_xn", [P, 2, D])
        a_xt = sb("a_xt", [P, 2, D])
        low_t = sb("low_t", [2 * LOW + 1, 2, P])
        clipped = sb("clipped", [P, 2, 2 * HM])
        slots = sb("slots", [P, 2, 2 * HM])
        rope_c = sb("rope_c", [P, 2 * D])
        rope_s = sb("rope_s", [P, 2 * D])
        qk = sb("qk", [P, 2, 2 * D])
        q_heads = sb("q_heads", [P, 2, H, P])
        k_t = sb("k_t", [P, 2, P])
        vg_all = sb("vg_all", [P, NC, 2 * D])
        gate_t = sb("gate_t", [P, D])
        gate_g = sb("gate_g", [P, 2, D])
        gates = sb("gates", [P, NC, D])
        state = sb("state", [P, 2, HM + 2 * 2 * DK])
        s_masked = sb("s_masked", [P, 2, H, P])
        slot_inv = sb("slot_inv", [P, 2, 2 * HM])
        logit = sb("logit", [P, HM])
        logit_max = sb("logit_max", [P, H])
        logit_c = sb("logit_c", [P, HM])
        prob = sb("prob", [P, HM])
        prob_sum = sb("prob_sum", [P, H])
        prob_inv = sb("prob_inv", [P, 2, H])
        pz = sb("pz", [P, HM])
        p_heads = sb("p_heads", [P, 2, 2, 2, P])
        vslot_t = sb("vslot_t", [P, 2, 2, P])
        a_masked = sb("a_masked", [P, H, P])
        o1 = sb("o1", [P, D])
        o_sq = sb("o_sq", [P, D])
        o_ss = sb("o_ss", [P, H])
        o_var = sb("o_var", [P, H])
        o_rstd = sb("o_rstd", [P, H])
        o2 = sb("o2", [P, D])
        o3 = sb("o3", [P, D])
        o_t = sb("o_t", [P, P])

        bank = [ctx.enter_context(nc.psum_tensor(f"bank{b}", [P, 512], F32)) for b in range(8)]
        gate_ps, up_ps, down_ps = [bank[0], bank[1]], [bank[2], bank[3]], [bank[4], bank[5]]
        xt_ps, router_ps = [bank[6], bank[7]], bank[7][:, 0:NC * ER]
        state_ps, sum_ps, qk_ps, slots_ps, s_ps, c_ps, in_ps, turn_ps = bank
        q_t_ps, k_t_ps = qk_ps[:, 0:P], qk_ps[:, P:2 * P]
        logit_ps, pz_t_ps = s_ps[:, 0:HM], s_ps[:, 0:HM]
        o_ps, y_ps = c_ps[:, 0:P], c_ps[:, P:2 * P]
        a_xt_ps, low_ps, vg_ps = in_ps[:, 0:P], in_ps[0:2 * LOW, P:2 * P], in_ps[:, 2 * P:4 * P]
        vslot_t_ps, o_t_ps = turn_ps[:, 0:HM], turn_ps[:, HM:HM + P]

        ident, tri, rest = cst[:, C_ID:C_ID + P], cst[:, C_TRI:C_TRI + P], cst[:, C_REST:C_REST + P]

        x_loaded = [sem(f"x_loaded{g}") for g in range(NG)]
        consts_loaded = sem("consts_loaded")
        router_loaded = sem("router_loaded")
        experts_loaded = [sem(f"expert{e}_loaded") for e in range(E)]
        attn_loaded = sem("attn_loaded")
        out_written = sem("out_written")
        wscaled, whi_done, wlo_done, wr_split = sem("wscaled"), sem("whi_done"), sem("wlo_done"), sem("wr_split")
        var_done, shift_done = sem("var_done"), sem("shift_done")
        stats_done, mv_done, rstd_done, xn_done = sem("stats_done"), sem("mv_done"), sem("rstd_done"), sem("xn_done")
        xt_turned, xt_hi_done, xt_lo_done = sem("xt_turned"), sem("xt_hi_done"), sem("xt_lo_done")
        router_done, z_done, score_done, route_step = sem("router_done"), sem("z_done"), sem("score_done"), sem("route_step")
        gate_done, up_done, silu_done, hmul_done = sem("gate_done"), sem("up_done"), sem("silu_done"), sem("hmul_done")
        hhi_done, hlo_done, down_done, added = sem("hhi_done"), sem("hlo_done"), sem("down_done"), sem("added")
        ones_set, shared_set, power_set = sem("ones_set"), sem("shared_set"), sem("power_set")
        names = ("a_xnd a_turned a_xt_copied projected low_done low_copied slots_done "
                 "clip_done slots_exp rope_parts qk_done qk_turned q_spread k_copied v_copied gate_tanh gate_raw gate_ready "
                 "s_done vslot_turned vslot_copied sums_done s_mask_done state_copied logits_done sums_inv back_done "
                 "logit_scaled max_done centred prob_done prob_summed pz_done pinv_done pz_turned p_spread "
                 "a_done a_mask_done o_done o1_done sq_done ss_done o_var_done orstd_done o2_done o3_done o_turned o_copied y_done y_added")
        S = {n: sem(n) for n in names.split()}

        block = ctx.enter_context(nc.Block())

        @block.sync
        def _(sp):
            sp.dma_start(x[:, 0:GT, :], x_d[0]).then_inc(x_loaded[0], 16)
            sp.dma_start(cst[:, :], consts).then_inc(consts_loaded, 16)
            sp.dma_start(wr[:, :], w_router).then_inc(router_loaded, 16)
            sp.dma_start(rbias[:, :], router_bias).then_inc(router_loaded, 16)
            for g in range(1, NG):
                sp.dma_start(x[:, g * GT:(g + 1) * GT, :], x_d[g]).then_inc(x_loaded[g], 16)
            for e in range(1, E, 2):
                sp.dma_start(wf[:, e, :], w_ffn[e]).then_inc(experts_loaded[e], 16)
            for g in range(NG):
                sp.wait_ge(added, 2 * (SPF + SPF - NG + g + 1))
                sp.dma_start(out_d[g], x[:, g * GT:(g + 1) * GT, :]).then_inc(out_written, 16)
            sp.wait_ge(out_written, 16 * NG)

        @block.scalar
        def _(act):
            for e in range(0, E, 2):
                act.dma_start(wf[:, e, :], w_ffn[e]).then_inc(experts_loaded[e], 16)
            for dst, src in ((wqkvg, w_qkvg), (wlow, w_low), (wslots, w_slots), (wo, w_out), (gn, gnorm)):
                act.dma_start(dst[:, :], src).then_inc(attn_loaded, 16)

            def tokens(f):
                for g in range(NG):
                    act.wait_ge(shift_done, NG * f + g + 1)
                    if NG * f + g >= 2:
                        act.wait_ge(xt_turned, NG * f + g - 1)
                    for c in range(GT):
                        i = act.activation(xn[:, g % 2, c, :], x[:, g * GT + c, :], ACT.Identity,
                                           bias=shift[:, g, c:c + 1], scale=rstd[:, g, c:c + 1])
                    i.then_inc(xn_done, 1)
                    act.wait_ge(xt_turned, NG * f + g + 1)
                    if f and g == 0:
                        act.wait_ge(up_done, IH * SPF)
                    act.activation(xt_hi[:, g * GW:(g + 1) * GW], xt_ps[g % 2][:, :], ACT.Copy,
                                   scale=XS).then_inc(xt_hi_done, 1)

            def step(f, e, g, first):
                s = SPF * f + NG * e + g
                for ih in range(IH):
                    u = IH * s + ih
                    if not (f == 0 and first and g == 0):
                        act.wait_ge(hmul_done, u - 1)
                    act.wait_ge(gate_done, u + 1)
                    act.activation(gate_s[:, ih, :], gate_ps[ih][:, :], ACT.Silu,
                                   scale=1.0 / (XS * WS)).then_inc(silu_done, 1)
                    act.wait_ge(hmul_done, u + 1)
                    if not (f == 0 and first):
                        act.wait_ge(down_done, 2 * (s - NG) + 2)
                    act.activation(h_hi[:, g, ih, :], h32[:, ih, :], ACT.Copy).then_inc(hhi_done, 1)

            def ffn(f):
                act.wait_ge(z_done, f + 1)
                act.activation(score[:, :, :], score_z[:, :, :], ACT.Sigmoid).then_inc(score_done, 1)
                for g in range(NG):
                    step(f, 0, g, True)
                with act.Fori(1, E) as e:
                    for g in range(NG):
                        step(f, e, g, False)

            def front_a(c, p, n):
                act.wait_ge(S["a_turned"], c + 1)
                if n >= 2:
                    act.wait_ge(S["low_done"], c - 1)
                act.activation(a_xt[:, p, :], a_xt_ps, ACT.Copy).then_inc(S["a_xt_copied"], 1)

            def front_b(c, p, n):
                act.wait_ge(S["low_done"], c + 1)
                if n >= 2:
                    act.wait_ge(S["slots_done"], c - 1)
                act.activation(low_t[0:2 * LOW, p, :], low_ps, ACT.Copy).then_inc(S["low_copied"], 1)

            def front_c(c, p, n):
                act.activation(vg_all[:, c, :], vg_ps, ACT.Copy).then_inc(S["v_copied"], 1)
                act.wait_ge(S["v_copied"], c + 1)
                if n >= 1:
                    act.wait_ge(S["gate_raw"], c)
                act.activation(gate_t[:, :], vg_all[:, c, D:2 * D], ACT.Tanh, scale=0.5).then_inc(S["gate_tanh"], 1)

            def front_d(c, p, n):
                act.wait_ge(S["clip_done"], c + 1)
                if n >= 2:
                    act.wait_ge(S["back_done"], c - 1)
                act.activation(slots[:, p, :], clipped[:, p, :], ACT.Exp).then_inc(S["slots_exp"], 1)

            def front_e(c, p, n):
                act.wait_ge(S["qk_turned"], c + 1)
                act.activation(k_t[:, p, :], k_t_ps, ACT.Copy).then_inc(S["k_copied"], 1)

            def mid_a(c, p, n):
                act.wait_ge(S["vslot_turned"], c + 1)
                if n >= 2:
                    act.wait_ge(S["a_done"], c - 1)
                act.activation(vslot_t[:, p, :, :], vslot_t_ps.rearrange("p (a b) -> p a b", a=2), ACT.Copy).then_inc(S["vslot_copied"], 1)

            def mid_b(c, p, n):
                if n >= 1:
                    act.wait_ge(S["back_done"], c)
                    if n >= 2:
                        act.wait_ge(S["o_done"], c - 1)
                    act.activation(state[:, p, :], state_ps[:, 0:HM + 4 * DK], ACT.Copy).then_inc(S["state_copied"], 1)

            def mid_c(c, p, n):
                act.wait_ge(S["centred"], c + 1)
                if n >= 1:
                    act.wait_ge(S["pz_done"], c)
                act.activation(prob[:, :], logit_c[:, :], ACT.Exp, scale=DK ** -0.5).then_inc(S["prob_done"], 1)

            def last_a(c, p, n):
                act.wait_ge(S["o_turned"], c + 1)
                if n >= 1:
                    act.wait_ge(S["y_done"], c)
                act.activation(o_t[:, :], o_t_ps, ACT.Copy).then_inc(S["o_copied"], 1)

            def attn_step(i, n):
                front, mid, last = stages(i, n)
                if mid:
                    mid_b(*mid)
                if front:
                    front_a(*front)
                if mid:
                    mid_a(*mid)
                if front:
                    front_b(*front)
                if front:
                    front_c(*front)
                if mid:
                    mid_c(*mid)
                if front:
                    front_d(*front)
                if front:
                    front_e(*front)
                if last:
                    last_a(*last)

            tokens(0)
            ffn(0)
            attention(act, attn_step)
            tokens(1)
            ffn(1)

        @block.gpsimd
        def _(pool):
            nc.gpsimd.memset(power[:, :], -0.5).then_inc(power_set, 1)
            pool.wait_ge(power_set, 1)

            def root(dst, src, n):
                if n:
                    pool.wait_ge(rstd_done, n)
                nc.gpsimd.tensor_scalar(var_e[:, 0:dst.shape[1]], src, EPS, None, ALU.add).then_inc(var_done, 1)
                pool.wait_ge(var_done, n + 1)
                nc.gpsimd.tensor_tensor(dst, var_e[:, 0:dst.shape[1]], power[:, 0:dst.shape[1]], ALU.pow).then_inc(rstd_done, 1)

            def tokens(n, f):
                for g in range(NG):
                    pool.wait_ge(mv_done, n + g + 1)
                    if f and g == 0:
                        pool.wait_ge(xn_done, NG)
                    root(rstd[:, g, :], mv[:, g, :, 1], n + g)

            tokens(0, 0)

            pool.wait_ge(router_loaded, 32)
            nc.gpsimd.tensor_scalar(wrs[:, :], wr[:, :], WS, None, ALU.mult).then_inc(wscaled, 1)
            pool.wait_ge(wscaled, 1)
            nc.gpsimd.tensor_copy(wr_hi[:, :], wrs[:, :]).then_inc(whi_done, 1)
            pool.wait_ge(whi_done, 1)
            nc.gpsimd.tensor_tensor(wr_lo[:, :], wrs[:, :], wr_hi[:, :], ALU.subtract).then_inc(wr_split, 1)
            for e in range(E):
                pool.wait_ge(experts_loaded[e], 16)
                if e:
                    pool.wait_ge(wlo_done, e)
                nc.gpsimd.tensor_scalar(wsc[:, :], wf[:, e, :], WS, None, ALU.mult).then_inc(wscaled, 1)
                pool.wait_ge(wscaled, e + 2)
                nc.gpsimd.tensor_copy(w_hi[:, e, :], wsc[:, :]).then_inc(whi_done, 1)
                pool.wait_ge(whi_done, e + 2)
                nc.gpsimd.tensor_tensor(w_lo[:, e, :], wsc[:, :], w_hi[:, e, :], ALU.subtract).then_inc(wlo_done, 1)

            def o_root(c, p, n):
                pool.wait_ge(S["o_var_done"], c + 1)
                if n >= 1:
                    pool.wait_ge(S["o3_done"], c)
                nc.gpsimd.tensor_tensor(o_rstd[:, :], o_var[:, :], power[:, 0:H], ALU.pow).then_inc(S["orstd_done"], 1)

            def gate_norm(c, p, n):
                pool.wait_ge(S["gate_raw"], c + 1)
                nc.gpsimd.tensor_tensor(gates[:, c, :], gate_g[:, p, :], gn[:, :], ALU.mult).then_inc(S["gate_ready"], 1)

            def o_gated(c, p, n):
                pool.wait_ge(S["o1_done"], c + 1)
                if n >= 1:
                    pool.wait_ge(S["o3_done"], c)
                pool.wait_ge(S["gate_ready"], c + 1)
                nc.gpsimd.tensor_tensor(o2[:, :], o1[:, :], gates[:, c, :], ALU.mult).then_inc(S["o2_done"], 1)

            def attn_step(i, n):
                front, mid, last = stages(i, n)
                if last:
                    o_gated(*last)
                if last:
                    o_root(*last)
                if front:
                    gate_norm(*front)

            pool.wait_ge(attn_loaded, 80)
            pool.wait_ge(mv_done, NG + 1)
            root(a_rstd[:, :], a_mv[:, :, 1], NG)
            attention(pool, attn_step)
            tokens(NG + 1, 1)

        @block.vector
        def _(dve):
            nc.vector.memset(low_t[2 * LOW:2 * LOW + 1, :, :], 1.0).then_inc(ones_set, 1)
            nc.vector.memset(wts[:, :, 0:1], 0.5 / (WS * HS)).then_inc(shared_set, 1)
            dve.wait_ge(consts_loaded, 16)

            def moments(f, g):
                m = (NG + 1) * f + g
                if f == 0:
                    dve.wait_ge(x_loaded[g], 16)
                elif g == 0:
                    dve.wait_ge(S["y_added"], NC)
                for c in range(GT):
                    i = nc.vector.bn_stats(stats[:, g, c, :], x[:, g * GT + c, :])
                i.then_inc(stats_done, 1)
                dve.wait_ge(stats_done, m + 1)
                for c in range(GT):
                    i = nc.vector.bn_aggr(mv[:, g, c, :], stats[:, g, c, :])
                i.then_inc(mv_done, 1)

            def centre(f, g):
                dve.wait_ge(rstd_done, (NG + 1) * f + g + 1)
                if f:
                    dve.wait_ge(xn_done, NG)
                nc.vector.scalar_tensor_tensor(shift[:, g, :], mv[:, g, :, 0], -1.0, rstd[:, g, :], ALU.mult,
                                               ALU.mult).then_inc(shift_done, 1)

            def low_part(f, g):
                dve.wait_ge(xt_hi_done, NG * f + g + 1)
                nc.vector.scalar_tensor_tensor(xt_lo[:, g * GW:(g + 1) * GW], xt_ps[g % 2][:, :], XS,
                                               xt_hi[:, g * GW:(g + 1) * GW], ALU.mult,
                                               ALU.subtract).then_inc(xt_lo_done, 1)

            def tokens(f):
                moments(f, 0)
                for g in range(NG):
                    if g + 1 < NG:
                        moments(f, g + 1)
                    centre(f, g)
                    if g:
                        low_part(f, g - 1)
                low_part(f, NG - 1)

            routed = [0]

            def chain(ins):
                routed[0] += 1
                ins.then_inc(route_step, 1)
                dve.wait_ge(route_step, routed[0])

            def route(f):
                dve.wait_ge(router_done, f + 1)
                dve.wait_ge(router_loaded, 32)
                nc.vector.scalar_tensor_tensor(score_z[:, :, :], router_ps.rearrange("p (c e) -> p c e", e=ER),
                                               1.0 / (XS * WS), rbias[:, :].unsqueeze(1).broadcast_to([P, NC, ER]), ALU.mult,
                                               ALU.add).then_inc(z_done, 1)
                dve.wait_ge(score_done, f + 1)
                for c in range(NC):
                    i = nc.vector.max(top[:, c, :], score[:, c, :])
                chain(i)
                for c in range(NC):
                    i = nc.vector.max_index(top_at[:, c, :], top[:, c, :], score[:, c, :])
                chain(i)
                nc.vector.tensor_copy(top_af[:, :, :], top_at[:, :, 0:2])
                chain(nc.vector.tensor_tensor(top_sum[:, :], top[:, :, 0], top[:, :, 1], ALU.add))
                chain(nc.vector.reciprocal(top_inv[:, :], top_sum[:, :]))
                chain(nc.vector.scalar_tensor_tensor(share[:, :, :], top[:, :, 0:2], 0.5 / (WS * HS),
                                                     top_inv[:, :].unsqueeze(2).broadcast_to([P, NC, 2]), ALU.mult, ALU.mult))
                for k in range(2):
                    i = nc.vector.tensor_tensor(pick[:, k, :, :], cst[:, C_IOTA:C_IOTA + ER].unsqueeze(1).broadcast_to([P, NC, ER]),
                                                top_af[:, :, k:k + 1].broadcast_to([P, NC, ER]), ALU.is_equal)
                chain(i)
                for k in range(2):
                    i = nc.vector.tensor_tensor(pick[:, k, :, :], pick[:, k, :, :],
                                                share[:, :, k:k + 1].broadcast_to([P, NC, ER]), ALU.mult)
                chain(i)
                chain(nc.vector.tensor_tensor(wts[:, :, 1:E], pick[:, 0, :, :], pick[:, 1, :, :], ALU.add))

            def add_half(f, e, g, j):
                s = SPF * f + NG * e + g
                dve.wait_ge(down_done, 2 * s + j + 1)
                for c in range(2 * j, 2 * j + 2):
                    t = g * GT + c
                    i = nc.vector.scalar_tensor_tensor(x[:, t, :], down_ps[j][:, c % 2 * P:(c % 2 + 1) * P],
                                                       wts[:, t, e:e + 1] if isinstance(e, int) else wts[:, t, bass.ds(e, 1)],
                                                       x[:, t, :], ALU.mult, ALU.add)
                i.then_inc(added, 1)

            def hidden(f, u, ih, first):
                dve.wait_ge(silu_done, u + 1)
                dve.wait_ge(up_done, u + 1)
                if not first:
                    dve.wait_ge(hlo_done, u - 1)
                nc.vector.scalar_tensor_tensor(h32[:, ih, :], up_ps[ih][:, :], HS / (XS * WS), gate_s[:, ih, :],
                                               ALU.mult, ALU.mult).then_inc(hmul_done, 1)

            def rest_of(u, g, ih):
                dve.wait_ge(hhi_done, u + 1)
                nc.vector.tensor_tensor(h_lo[:, g, ih, :], h32[:, ih, :], h_hi[:, g, ih, :],
                                        ALU.subtract).then_inc(hlo_done, 1)

            def step(f, e, g, e2):
                for ih in range(IH):
                    u = IH * (SPF * f + NG * e + g) + ih
                    hidden(f, u, ih, f == 0 and e2 is None and g == 0)
                    if not (e2 is None and g == 0 and ih == 0):
                        rest_of(u - 1, (g - (ih == 0)) % NG, 1 - ih)
                    if not (e2 is None and g < 2):
                        add_half(f, e if g >= 2 else e2, (g - 2) % NG, ih)

            def ffn(f):
                for g in range(NG):
                    step(f, 0, g, None)
                with dve.Fori(1, E) as e:
                    for g in range(NG):
                        step(f, e, g, e - 1)
                rest_of(IH * SPF * (f + 1) - 1, NG - 1, 1)
                for g in (NG - 2, NG - 1):
                    for j in range(2):
                        add_half(f, E - 1, g, j)

            def all_stats():
                dve.wait_ge(added, 2 * SPF)
                for c in range(NC):
                    i = nc.vector.bn_stats(a_st[:, c, :], x[:, c, :])
                i.then_inc(stats_done, 1)
                dve.wait_ge(stats_done, NG + 1)
                for c in range(NC):
                    i = nc.vector.bn_aggr(a_mv[:, c, :], a_st[:, c, :])
                i.then_inc(mv_done, 1)
                dve.wait_ge(rstd_done, NG + 1)

            def norm_x(c, p, n):
                if n >= 2:
                    dve.wait_ge(S["a_turned"], c - 1)
                nc.vector.tensor_scalar(a_xn[:, p, :], x[:, c, :], a_mv[:, c, 0:1], a_rstd[:, bass.ds(c, 1)], ALU.subtract,
                                        ALU.mult).then_inc(S["a_xnd"], 1)

            def rope(c, p, n):
                dve.wait_ge(S["projected"], c + 1)
                half = DK // 2
                src = qk_ps[:, 0:2 * D].rearrange("p (a b j) -> p a b j", b=2, j=half)
                dst = rope_s[:, :].rearrange("p (a b j) -> p a b j", b=2, j=half)
                cos = cst[:, bass.ds(C_COS + c * half, half)]
                sin = cst[:, bass.ds(C_SIN + c * half, half)]
                nc.vector.tensor_tensor(rope_c[:, :].rearrange("p (a j) -> p a j", j=half),
                                        qk_ps[:, 0:2 * D].rearrange("p (a j) -> p a j", j=half),
                                        cos.unsqueeze(1).broadcast_to([P, 4 * H, half]), ALU.mult)
                nc.vector.tensor_tensor(dst[:, :, 0, :], src[:, :, 1, :],
                                        sin.unsqueeze(1).broadcast_to([P, 2 * H, half]), ALU.mult)
                nc.vector.tensor_tensor(dst[:, :, 1, :], src[:, :, 0, :],
                                        sin.unsqueeze(1).broadcast_to([P, 2 * H, half]), ALU.mult).then_inc(S["rope_parts"], 1)
                dve.wait_ge(S["rope_parts"], c + 1)
                if n >= 2:
                    dve.wait_ge(S["back_done"], c - 1)
                tc_ = rope_c[:, :].rearrange("p (a b j) -> p a b j", b=2, j=half)
                to = qk[:, p, :].rearrange("p (a b j) -> p a b j", b=2, j=half)
                nc.vector.tensor_tensor(to[:, :, 0, :], tc_[:, :, 0, :], dst[:, :, 0, :], ALU.subtract)
                nc.vector.tensor_tensor(to[:, :, 1, :], tc_[:, :, 1, :], dst[:, :, 1, :], ALU.add).then_inc(S["qk_done"], 1)

            def gate(c, p, n):
                dve.wait_ge(S["gate_tanh"], c + 1)
                if n >= 2:
                    dve.wait_ge(S["gate_ready"], c - 1)
                nc.vector.scalar_tensor_tensor(gate_g[:, p, :], gate_t[:, :], 1.0, vg_all[:, c, D:2 * D], ALU.add,
                                               ALU.mult).then_inc(S["gate_raw"], 1)

            def clip(c, p, n):
                dve.wait_ge(S["slots_done"], c + 1)
                if n >= 2:
                    dve.wait_ge(S["slots_exp"], c - 1)
                nc.vector.tensor_scalar(clipped[:, p, :], slots_ps[:, :], CLAMP, -CLAMP, ALU.min,
                                        ALU.max).then_inc(S["clip_done"], 1)

            def spread_q(c, p, n):
                dve.wait_ge(S["k_copied"], c + 1)
                if n >= 2:
                    dve.wait_ge(S["logits_done"], c - 1)
                nc.vector.tensor_tensor(q_heads[:, p, :, :], q_t_ps.unsqueeze(1).broadcast_to([P, H, P]),
                                        cst[:, C_HEAD:C_HEAD + H].unsqueeze(2).broadcast_to([P, H, P]),
                                        ALU.mult).then_inc(S["q_spread"], 1)

            def mask_s(c, p, n):
                dve.wait_ge(S["s_done"], c + 1)
                if n >= 2:
                    dve.wait_ge(S["logits_done"], c - 1)
                nc.vector.tensor_tensor(s_masked[:, p, :, :], s_ps[:, :].rearrange("p (h t) -> p h t", h=H),
                                        tri.unsqueeze(1).broadcast_to([P, H, P]), ALU.mult).then_inc(S["s_mask_done"], 1)

            def invert(c, p, n):
                dve.wait_ge(S["sums_done"], c + 1)
                nc.vector.reciprocal(slot_inv[:, p, :], sum_ps[:, :]).then_inc(S["sums_inv"], 1)

            def soft_a(c, p, n):
                dve.wait_ge(S["logits_done"], c + 1)
                dve.wait_ge(S["sums_inv"], c + 1)
                nc.vector.tensor_tensor(logit[:, :], logit_ps, slot_inv[:, p, 0:HM], ALU.mult).then_inc(S["logit_scaled"], 1)
                dve.wait_ge(S["logit_scaled"], c + 1)
                lv = logit[:, :].rearrange("p (h m) -> p h m", h=H)
                nc.vector.reduce_max(logit_max[:, :], lv, AX_X).then_inc(S["max_done"], 1)
                dve.wait_ge(S["max_done"], c + 1)
                if n >= 1:
                    dve.wait_ge(S["prob_done"], c)
                nc.vector.tensor_tensor(logit_c[:, :].rearrange("p (h m) -> p h m", h=H), lv,
                                        logit_max[:, :].unsqueeze(2).broadcast_to([P, H, M]), ALU.subtract).then_inc(S["centred"], 1)

            def soft_b(c, p, n):
                dve.wait_ge(S["prob_done"], c + 1)
                nc.vector.reduce_sum(prob_sum[:, :], prob[:, :].rearrange("p (h m) -> p h m", h=H), AX_X).then_inc(S["prob_summed"], 1)
                if n >= 1:
                    dve.wait_ge(S["pz_turned"], c)
                nc.vector.tensor_tensor(pz[:, :], prob[:, :], slot_inv[:, p, HM:2 * HM], ALU.mult).then_inc(S["pz_done"], 1)
                dve.wait_ge(S["prob_summed"], c + 1)
                nc.vector.reciprocal(prob_inv[:, p, :], prob_sum[:, :]).then_inc(S["pinv_done"], 1)

            def spread_p(c, p, n):
                dve.wait_ge(S["pz_turned"], c + 1)
                if n >= 2:
                    dve.wait_ge(S["o_done"], c - 1)
                for a in range(2):
                    i = nc.vector.tensor_tensor(p_heads[:, p, a, :, :], pz_t_ps[:, a * P:(a + 1) * P].unsqueeze(1).broadcast_to([P, 2, P]),
                                                cst[:, C_PAIR:C_PAIR + 2].unsqueeze(2).broadcast_to([P, 2, P]), ALU.mult)
                i.then_inc(S["p_spread"], 1)

            def mask_a(c, p, n):
                dve.wait_ge(S["a_done"], c + 1)
                if n >= 1:
                    dve.wait_ge(S["o_done"], c)
                nc.vector.tensor_tensor(a_masked[:, :, :], c_ps[:, :].rearrange("p (h t) -> p h t", h=H),
                                        tri.unsqueeze(1).broadcast_to([P, H, P]), ALU.mult).then_inc(S["a_mask_done"], 1)

            def norm_a(c, p, n):
                dve.wait_ge(S["o_done"], c + 1)
                dve.wait_ge(S["pinv_done"], c + 1)
                if n >= 1:
                    dve.wait_ge(S["o2_done"], c)
                nc.vector.tensor_tensor(o1[:, :].rearrange("p (h d) -> p h d", h=H), o_ps.rearrange("p (h d) -> p h d", h=H),
                                        prob_inv[:, p, :].unsqueeze(2).broadcast_to([P, H, DK]), ALU.mult).then_inc(S["o1_done"], 1)
                dve.wait_ge(S["o1_done"], c + 1)
                nc.vector.tensor_tensor(o_sq[:, :], o1[:, :], o1[:, :], ALU.mult).then_inc(S["sq_done"], 1)
                dve.wait_ge(S["sq_done"], c + 1)
                nc.vector.reduce_sum(o_ss[:, :], o_sq[:, :].rearrange("p (h d) -> p h d", h=H), AX_X).then_inc(S["ss_done"], 1)
                dve.wait_ge(S["ss_done"], c + 1)
                if n >= 1:
                    dve.wait_ge(S["orstd_done"], c)
                nc.vector.tensor_scalar(o_var[:, :], o_ss[:, :], DK * EPS, None, ALU.add).then_inc(S["o_var_done"], 1)

            def norm_b(c, p, n):
                dve.wait_ge(S["orstd_done"], c + 1)
                dve.wait_ge(S["o2_done"], c + 1)
                if n >= 1:
                    dve.wait_ge(S["o_turned"], c)
                nc.vector.scalar_tensor_tensor(o3[:, :].rearrange("p (h d) -> p h d", h=H), o2[:, :].rearrange("p (h d) -> p h d", h=H),
                                               0.5 * DK ** 0.5, o_rstd[:, :].unsqueeze(2).broadcast_to([P, H, DK]), ALU.mult,
                                               ALU.mult).then_inc(S["o3_done"], 1)

            def add_y(c, p, n):
                dve.wait_ge(S["y_done"], c + 1)
                nc.vector.tensor_tensor(x[:, c, :], y_ps, x[:, c, :], ALU.add).then_inc(S["y_added"], 1)

            def attn_step(i, n):
                front, mid, last = stages(i, n)
                if front:
                    norm_x(*front)
                if last:
                    mask_a(*last)
                if mid:
                    mask_s(*mid)
                if mid:
                    invert(*mid)
                if front:
                    rope(*front)
                if last:
                    norm_a(*last)
                if mid:
                    soft_a(*mid)
                if front:
                    gate(*front)
                if front:
                    clip(*front)
                if last:
                    norm_b(*last)
                if mid:
                    soft_b(*mid)
                if front:
                    spread_q(*front)
                if mid:
                    spread_p(*mid)
                if last:
                    add_y(*last)

            tokens(0)
            route(0)
            ffn(0)
            all_stats()
            attention(dve, attn_step)
            tokens(1)
            route(1)
            ffn(1)

        @block.tensor
        def _(pe):
            mm = nc.tensor.matmul

            def tokens(f):
                for g in range(NG):
                    n = NG * f + g
                    pe.wait_ge(xn_done, n + 1)
                    if f and g == 0:
                        pe.wait_ge(S["y_added"], NC)
                    if g >= 2:
                        pe.wait_ge(xt_lo_done, n - 1)
                    for c in range(GT):
                        i = nc.tensor.transpose(xt_ps[g % 2][:, c * P:(c + 1) * P], xn[:, g % 2, c, :], ident)
                    i.then_inc(xt_turned, 1)

            def router(f):
                pe.wait_ge(wr_split, 1)
                pe.wait_ge(xt_lo_done, NG * (f + 1))
                if f:
                    pe.wait_ge(S["s_mask_done"], NC)
                for c in range(NC):
                    ts = slice(c * P, (c + 1) * P)
                    dst = router_ps[:, c * ER:(c + 1) * ER]
                    mm(dst, xt_hi[:, ts], wr_hi[:, :], start=True, stop=False)
                    mm(dst, xt_hi[:, ts], wr_lo[:, :], start=False, stop=False)
                    i = mm(dst, xt_lo[:, ts], wr_hi[:, :], start=False, stop=True)
                i.then_inc(router_done, 1)

            def wcols(parts, e, at, n):
                return parts[:, e, at:at + n]

            def down_half(f, e, g, j):
                s = SPF * f + NG * e + g
                pe.wait_ge(hlo_done, 2 * s + 2)
                if not (f == 0 and isinstance(e, int) and e == 0 and g == 0):
                    pe.wait_ge(added, 2 * (s - 1) + j + 1)
                for c in range(2 * j, 2 * j + 2):
                    dst = down_ps[j][:, c % 2 * P:(c % 2 + 1) * P]
                    k = 0
                    for ih in range(IH):
                        at = 2 * I + ih * D
                        for hp, wp in ((h_hi, w_hi), (h_hi, w_lo), (h_lo, w_hi)):
                            i = mm(dst, hp[:, g, ih, c * P:(c + 1) * P], wcols(wp, e, at, D),
                                   start=(k == 0), stop=(k == 3 * IH - 1))
                            k += 1
                i.then_inc(down_done, 1)

            def unit(f, e, g, ih, first):
                u = IH * (SPF * f + NG * e + g) + ih
                if not (f == 0 and first):
                    pe.wait_ge(hmul_done, u - 1)
                ts = slice(g * GW, (g + 1) * GW)
                for at, ps, done in ((ih * P, gate_ps[ih], gate_done), (I + ih * P, up_ps[ih], up_done)):
                    mm(ps[:, :], wcols(w_hi, e, at, P), xt_hi[:, ts], start=True, stop=False)
                    mm(ps[:, :], wcols(w_lo, e, at, P), xt_hi[:, ts], start=False, stop=False)
                    mm(ps[:, :], wcols(w_hi, e, at, P), xt_lo[:, ts], start=False, stop=True).then_inc(done, 1)

            def ffn(f):
                pe.wait_ge(wlo_done, 1)
                for g in range(NG):
                    unit(f, 0, g, 0, g == 0)
                    if g >= 2:
                        down_half(f, 0, g - 2, 1)
                    unit(f, 0, g, 1, g == 0)
                    if g >= 1:
                        down_half(f, 0, g - 1, 0)
                with pe.Fori(1, E) as e:
                    if f == 0:
                        pe.wait_ge(wlo_done, e + 1)
                    for g in range(NG):
                        unit(f, e, g, 0, False)
                        down_half(f, e if g >= 2 else e - 1, (g - 2) % NG, 1)
                        unit(f, e, g, 1, False)
                        down_half(f, e if g >= 1 else e - 1, (g - 1) % NG, 0)
                down_half(f, E - 1, NG - 2, 1)
                for j in range(2):
                    down_half(f, E - 1, NG - 1, j)

            def turn_x(c, p, n):
                pe.wait_ge(S["a_xnd"], c + 1)
                if n >= 1:
                    pe.wait_ge(S["low_copied"], c)
                    pe.wait_ge(S["v_copied"], c)
                nc.tensor.transpose(a_xt_ps, a_xn[:, p, :], ident).then_inc(S["a_turned"], 1)

            def project(c, p, n):
                pe.wait_ge(S["a_xt_copied"], c + 1)
                if n >= 1:
                    pe.wait_ge(S["q_spread"], c)
                    pe.wait_ge(S["k_copied"], c)
                mm(low_ps, wlow[:, :], a_xt[:, p, :], start=True, stop=True)
                mm(vg_ps, a_xt[:, p, :], wqkvg[:, 2 * D:], start=True, stop=True).then_inc(S["low_done"], 1)
                mm(qk_ps[:, 0:2 * D], a_xt[:, p, :], wqkvg[:, 0:2 * D], start=True, stop=True).then_inc(S["projected"], 1)

            def slot_logits(c, p, n):
                pe.wait_ge(S["low_copied"], c + 1)
                if n >= 1:
                    pe.wait_ge(S["clip_done"], c)
                mm(slots_ps[:, :], low_t[:, p, :], wslots[:, :], start=True, stop=True).then_inc(S["slots_done"], 1)

            def turn_qk(c, p, n):
                pe.wait_ge(S["qk_done"], c + 1)
                nc.tensor.transpose(q_t_ps, qk[:, p, 0:D], ident)
                nc.tensor.transpose(k_t_ps, qk[:, p, D:2 * D], ident).then_inc(S["qk_turned"], 1)

            def scores(c, p, n):
                pe.wait_ge(S["k_copied"], c + 1)
                pe.wait_ge(S["q_spread"], c + 1)
                if n >= 1:
                    pe.wait_ge(S["p_spread"], c)
                mm(s_ps[:, :], k_t[:, p, :], q_heads[:, p, :, :], start=True, stop=True).then_inc(S["s_done"], 1)

            def turn_v(c, p, n):
                pe.wait_ge(S["slots_exp"], c + 1)
                if n >= 1:
                    pe.wait_ge(S["vslot_copied"], c)
                if n >= 2:
                    pe.wait_ge(S["o_copied"], c - 1)
                for a in range(2):
                    i = nc.tensor.transpose(vslot_t_ps[:, a * P:(a + 1) * P], slots[:, p, HM + a * P:HM + (a + 1) * P], ident)
                i.then_inc(S["vslot_turned"], 1)

            def running(c, p, n):
                mm(sum_ps[:, :], tri, slots[:, p, :], start=(n == 0), stop=True, skip_group_check=True).then_inc(S["sums_done"], 1)

            def logits(c, p, n):
                pe.wait_ge(S["s_mask_done"], c + 1)
                if n >= 1:
                    pe.wait_ge(S["state_copied"], c)
                for h in range(H):
                    hs = slice(h * M, (h + 1) * M)
                    if n >= 1:
                        mm(logit_ps[:, hs], q_heads[:, p, h, :], state[:, p, hs], start=True, stop=False)
                    i = mm(logit_ps[:, hs], s_masked[:, p, h, :], slots[:, p, hs], start=(n == 0), stop=True)
                i.then_inc(S["logits_done"], 1)

            def add_state(c, p, n):
                pe.wait_ge(S["sums_inv"], c + 1)
                mm(sum_ps[:, :], rest, slots[:, p, :], start=False, stop=True, skip_group_check=True)
                if n >= 1:
                    pe.wait_ge(S["state_copied"], c)
                pe.wait_ge(S["v_copied"], c + 1)
                mm(state_ps[:, 0:HM], qk[:, p, D:2 * D], slots[:, p, 0:HM], start=(n == 0), stop=True, skip_group_check=True)
                for a in range(2):
                    i = mm(state_ps[:, HM + a * 2 * DK:HM + (a + 1) * 2 * DK], slots[:, p, HM + a * P:HM + (a + 1) * P],
                           vg_all[:, c, a * 2 * DK:(a + 1) * 2 * DK], start=False, stop=True, skip_group_check=True)
                i.then_inc(S["back_done"], 1)

            def turn_p(c, p, n):
                pe.wait_ge(S["pz_done"], c + 1)
                pe.wait_ge(S["logit_scaled"], c + 1)
                for a in range(2):
                    i = nc.tensor.transpose(pz_t_ps[:, a * P:(a + 1) * P], pz[:, a * P:(a + 1) * P], ident)
                i.then_inc(S["pz_turned"], 1)

            def weights_a(c, p, n):
                pe.wait_ge(S["p_spread"], c + 1)
                pe.wait_ge(S["vslot_copied"], c + 1)
                if n >= 1:
                    pe.wait_ge(S["y_added"], c)
                for a in range(2):
                    i = mm(c_ps[:, a * 2 * P:(a + 1) * 2 * P], vslot_t[:, p, a, :], p_heads[:, p, a, :, :], start=True, stop=True)
                i.then_inc(S["a_done"], 1)

            def outputs(c, p, n):
                pe.wait_ge(S["a_mask_done"], c + 1)
                for h in range(H):
                    hs = slice(h * DK, (h + 1) * DK)
                    if n >= 1:
                        mm(o_ps[:, hs], p_heads[:, p, h // 2, h % 2, :], state[:, p, HM + h * DK:HM + (h + 1) * DK],
                           start=True, stop=False)
                    i = mm(o_ps[:, hs], a_masked[:, h, :], vg_all[:, c, hs], start=(n == 0), stop=True)
                i.then_inc(S["o_done"], 1)

            def turn_o(c, p, n):
                pe.wait_ge(S["o3_done"], c + 1)
                pe.wait_ge(S["vslot_copied"], c + 2 if n + 2 <= NC else NC)
                nc.tensor.transpose(o_t_ps, o3[:, :], ident).then_inc(S["o_turned"], 1)

            def out_proj(c, p, n):
                pe.wait_ge(S["o_copied"], c + 1)
                mm(y_ps, o_t[:, :], wo[:, :], start=True, stop=True).then_inc(S["y_done"], 1)

            def attn_step(i, n):
                front, mid, last = stages(i, n)
                if last:
                    weights_a(*last)
                if front:
                    turn_x(*front)
                if mid:
                    scores(*mid)
                if front:
                    project(*front)
                if mid:
                    turn_v(*mid)
                if mid:
                    running(*mid)
                if last:
                    outputs(*last)
                if mid:
                    logits(*mid)
                if front:
                    slot_logits(*front)
                if mid:
                    add_state(*mid)
                if front:
                    turn_qk(*front)
                if last:
                    turn_o(*last)
                if mid:
                    turn_p(*mid)
                if last:
                    out_proj(*last)

            pe.wait_ge(consts_loaded, 16)
            tokens(0)
            router(0)
            ffn(0)
            pe.wait_ge(attn_loaded, 80)
            pe.wait_ge(ones_set, 1)
            pe.wait_ge(added, 2 * SPF)
            attention(pe, attn_step)
            tokens(1)
            router(1)
            ffn(1)


def stages(i, n):
    return [(i - late, (n - late) % 2, n - late) if 0 <= n - late < NC else None
            for late in range(3)]


def attention(eng, step):
    for i in range(4):
        step(i, i)
    with eng.Fori(2, NC // 2) as k:
        step(2 * k, 4)
        step(2 * k + 1, 5)
    for i in range(NC, NC + 2):
        step(i, i)


def kernel(**inputs):
    import numpy as _np
    import concourse.bacc as _bacc
    from concourse import mybir as _mybir
    from concourse.bass_utils import run_bass_kernel_spmd as _run

    a = {k.replace("L0_", ""): _np.asarray(v) for k, v in inputs.items()}
    gate = _np.concatenate([a["ffn_shared_gate"].T[None], a["ffn_gate_w"]])
    up = _np.concatenate([a["ffn_shared_up"].T[None], a["ffn_up_w"]])
    down = _np.concatenate([a["ffn_shared_down"].T[None], a["ffn_down_w"]])
    down = down.reshape(E, IH, P, D).transpose(0, 2, 1, 3).reshape(E, P, IH * D)
    slots = _np.zeros((2 * LOW + 1, 2 * HM), _np.float32)
    slots[0:LOW, 0:HM] = a["attn_sk_w2"]
    slots[LOW:2 * LOW, HM:] = a["attn_sv_w2"]
    slots[2 * LOW, 0:HM] = a["attn_sk_b2"]
    slots[2 * LOW, HM:] = a["attn_sv_b2"]
    arrays = {
        "x": a["attn_hidden_states"].reshape(T, D),
        "consts": constants(),
        "w_ffn": _np.concatenate([gate, up, down], axis=2),
        "w_router": a["ffn_router_w"].T,
        "router_bias": _np.broadcast_to(a["ffn_routing_bias"], (P, ER)),
        "w_qkvg": _np.concatenate([a["attn_Wq"], a["attn_Wk"], a["attn_Wv"], a["attn_Wg"]], axis=1),
        "w_low": _np.concatenate([a["attn_sk_w1"], a["attn_sv_w1"]], axis=1),
        "w_slots": slots,
        "w_out": a["attn_Wo"],
        "gnorm": _np.broadcast_to(_np.tile(a["attn_gnorm_w"], H), (P, D)),
    }
    nc = _bacc.Bacc("TRN2", target_bir_lowering=False, num_devices=1)
    arrays = {f"in_{k}": _np.ascontiguousarray(v) for k, v in arrays.items()}
    args = [nc.dram_tensor(k, v.shape, _mybir.dt.from_np(v.dtype), kind="ExternalInput").ap() for k, v in arrays.items()]
    args.append(nc.dram_tensor("out_dram", (T, D), _mybir.dt.float32, kind="ExternalOutput").ap())
    macaron_kernel(nc, *args)
    r = _run(nc, [arrays], core_ids=[0])
    return r.results[0]["out_dram"].reshape(1, T, D)
```

```python
from contextlib import ExitStack

import numpy as np
import concourse.bass as bass
from concourse import mybir

ALU = mybir.AluOpType
ACT = mybir.ActivationFunctionType
F32 = mybir.dt.float32
F16 = mybir.dt.float16
BF16 = mybir.dt.bfloat16
U32 = mybir.dt.uint32
AX_X = mybir.AxisListType.X

P = 128
T = 2048
D = 128
NC = T // P
GT = 4
NG = NC // GT
GW = GT * P
ER = 8
E = ER + 1
I = 256
IH = I // P
EW = 3 * I
H = 4
DK = D // H
M = 64
LOW = 16
HM = H * M
EPS = 1e-5
CLAMP = 32.0
XS = 64.0
WS = 64.0
HS = 16.0
WF = 3
SPF = NG * E

C_ID = 0
C_TRI = C_ID + P
C_REST = C_TRI + P
C_HEAD = C_REST + P
C_PAIR = C_HEAD + H
C_IOTA = C_PAIR + 2
C_COS = C_IOTA + ER
C_SIN = C_COS + NC * DK // 2
C_END = C_SIN + NC * DK // 2


def constants():
    half = DK // 2
    inv = np.float32(1.0) / np.float32(10000.0) ** (np.arange(half, dtype=np.float32) / np.float32(half))
    angle = np.arange(T, dtype=np.float32)[:, None] * inv.astype(np.float32)[None, :]
    row = np.arange(P)
    out = np.zeros((P, C_END), np.float32)
    out[:, C_ID:C_ID + P] = np.eye(P)
    out[:, C_TRI:C_TRI + P] = row[:, None] <= row[None, :]
    out[:, C_REST:C_REST + P] = row[:, None] > row[None, :]
    out[:, C_HEAD:C_HEAD + H] = row[:, None] // DK == np.arange(H)[None, :]
    out[:, C_PAIR:C_PAIR + 2] = -1.0 * (row[:, None] // M == np.arange(2)[None, :])
    out[:, C_IOTA:C_IOTA + ER] = np.arange(ER)[None, :]
    for at, f in ((C_COS, np.cos), (C_SIN, np.sin)):
        table = (f(angle).astype(np.float32) / np.float32(XS * WS)).reshape(NC, P, half).transpose(1, 0, 2)
        out[:, at:at + NC * half] = table.reshape(P, NC * half)
    return out


def macaron_kernel(nc, x_in, consts, w_ffn, w_router, router_bias, w_qkvg, w_low, w_slots, w_out, gnorm, out):
    x_d = x_in.rearrange("(g c p) d -> g p c d", p=P, c=GT)
    out_d = out.rearrange("(g c p) d -> g p c d", p=P, c=GT)

    with ExitStack() as ctx:
        def sb(name, shape, dt=F32):
            return ctx.enter_context(nc.sbuf_tensor(name, shape, dt))

        def sem(name):
            return ctx.enter_context(nc.semaphore(name))

        x = sb("x", [P, NC, D])
        cst = sb("cst", [P, C_END])
        wf = sb("wf", [P, WF, EW])
        wsc = sb("wsc", [P, EW])
        w_hi = sb("w_hi", [P, E, EW], F16)
        w_lo = sb("w_lo", [P, E, EW], F16)
        wr = sb("wr", [P, ER])
        wrs = sb("wrs", [P, ER])
        wr_hi = sb("wr_hi", [P, ER], F16)
        wr_lo = sb("wr_lo", [P, ER], F16)
        rbias = sb("rbias", [P, ER])
        wqkvg = sb("wqkvg", [P, 4 * D])
        wlow = sb("wlow", [P, 2 * LOW])
        wqkvg_hi = sb("wqkvg_hi", [P, 4 * D], F16)
        wqkvg_lo = sb("wqkvg_lo", [P, 4 * D], F16)
        wlow_hi = sb("wlow_hi", [P, 2 * LOW], F16)
        wlow_lo = sb("wlow_lo", [P, 2 * LOW], F16)
        wslots_hi = sb("wslots_hi", [P, 2 * HM], F16)
        wslots_lo = sb("wslots_lo", [P, 2 * HM], F16)
        tri16 = sb("tri16", [P, P], BF16)
        rest16 = sb("rest16", [P, P], BF16)
        head16 = sb("head16", [P, H, P], F16)
        zero16 = sb("zero16", [P, HM + 4 * DK], F16)
        ident16 = sb("ident16", [P, P], F16)
        wslots = sb("wslots", [P, 2 * HM])
        wo = sb("wo", [P, D])
        gn = sb("gn", [P, D])
        stats = sb("stats", [P, NG, GT, 6])
        mv = sb("mv", [P, NG, GT, 2])
        rstd = sb("rstd", [P, NG, GT])
        shift = sb("shift", [P, NG, GT])
        xn = sb("xn", [P, 2, GT, D])
        xt_hi = sb("xt_hi", [P, T], F16)
        xt_lo = sb("xt_lo", [P, T], F16)
        score_z = sb("score_z", [P, NC, ER])
        score = sb("score", [P, NC, ER])
        top = sb("top", [P, NC, 8])
        top_at = sb("top_at", [P, NC, 8], U32)
        top_af = sb("top_af", [P, NC, 2])
        top_sum = sb("top_sum", [P, NC])
        top_inv = sb("top_inv", [P, NC])
        share = sb("share", [P, NC, 2])
        pick = sb("pick", [P, 2, NC, ER])
        wts = sb("wts", [P, NC, E])
        gate_s = sb("gate_s", [P, IH, GW])
        h32 = sb("h32", [P, IH, GW])
        h_hi = sb("h_hi", [P, NG, IH, GW], F16)
        h_lo = sb("h_lo", [P, NG, IH, GW], F16)
        low_hi = sb("low_hi", [P, T], F16)
        low_lo = sb("low_lo", [P, T], F16)
        clipped = sb("clipped", [P, 2, 2 * HM])
        slots = sb("slots", [P, 2, 2 * HM])
        rope_c = sb("rope_c", [P, 2 * D])
        rope_s = sb("rope_s", [P, 2 * D])
        slot_b1 = sb("slot_b1", [P, 2, 2 * HM], BF16)
        slot_r = sb("slot_r", [P, 2 * HM])
        slot_b2 = sb("slot_b2", [P, 2, 2 * HM], BF16)
        slot_b3 = sb("slot_b3", [P, 2, 2 * HM], BF16)
        qk = sb("qk", [P, 2, 2 * D])
        qk_hi = sb("qk_hi", [P, 2 * D], F16)
        qk_lo = sb("qk_lo", [P, 2 * D], F16)
        qk_t = sb("qk_t", [P, 2, 4, P], F16)
        q_t = sb("q_t", [P, 2, P])
        v_all = sb("v_all", [P, NC, D])
        gate_raw = sb("gate_raw", [P, NC, D])
        gates = sb("gates", [P, NC, D])
        state = sb("state", [P, 2, HM + 2 * 2 * DK])
        s_masked = sb("s_masked", [P, 2, H, P])
        slot_inv = sb("slot_inv", [P, 2, 2 * HM])
        slot_ln = sb("slot_ln", [P, 2 * HM])
        slot_i0 = sb("slot_i0", [P, 2 * HM])
        slot_zi = sb("slot_zi", [P, 2 * HM])
        logit = sb("logit", [P, HM])
        logit_min = sb("logit_min", [P, H])
        logit_c = sb("logit_c", [P, HM])
        prob = sb("prob", [P, HM])
        prob_sum = sb("prob_sum", [P, H])
        prob_inv = sb("prob_inv", [P, 2, H])
        pz = sb("pz", [P, HM])
        q_heads = sb("q_heads", [P, 2, 2, H, P], F16)
        p_t = sb("p_t", [P, 2, 2, P])
        vslot_t = sb("vslot_t", [P, 2, 2, P])
        a_masked = sb("a_masked", [P, H, P])
        o1 = sb("o1", [P, D])
        o_sq = sb("o_sq", [P, D])
        o_ss = sb("o_ss", [P, H])
        o_var = sb("o_var", [P, H])
        o_rstd = sb("o_rstd", [P, H])
        var_e = sb("var_e", [P, NC])
        power = sb("power", [P, NC])
        o2 = sb("o2", [P, D])
        o3 = sb("o3", [P, D])
        o_t = sb("o_t", [P, P])

        bank = [ctx.enter_context(nc.psum_tensor(f"bank{b}", [P, 512], F32)) for b in range(8)]
        gate_ps, up_ps, down_ps = [bank[0], bank[1]], [bank[2], bank[3]], [bank[4], bank[5]]
        xt_ps, router_ps = [bank[6], bank[7]], bank[7][:, 0:NC * ER]
        low_ps, v_ps, g_ps = [b[0:2 * LOW, :] for b in bank[0:2]], bank[2:4], bank[4:6]
        state_ps, sum_ps, qk_ps, slots_ps, s_ps, c_ps, vturn_ps, oturn_ps = bank
        q_t_ps = qk_ps[:, 0:P]
        qk_t_ps = qk_ps[:, P:3 * P].bitcast(F16)
        logit_ps, o_ps = s_ps[:, 0:HM], c_ps[:, 0:P]
        vslot_t_ps, pz_t_ps = vturn_ps[:, 0:HM], vturn_ps[:, HM:2 * HM]
        o_t_ps, y_ps = oturn_ps[:, 0:P], oturn_ps[:, P:2 * P]

        ident, tri, rest = cst[:, C_ID:C_ID + P], cst[:, C_TRI:C_TRI + P], cst[:, C_REST:C_REST + P]

        x_loaded = [sem(f"x_loaded{g}") for g in range(NG)]
        consts_loaded = sem("consts_loaded")
        router_loaded = sem("router_loaded")
        experts_loaded = [sem(f"expert{e}_loaded") for e in range(E)]
        attn_loaded = sem("attn_loaded")
        out_written = sem("out_written")
        wscaled, whi_done, wlo_done, wr_split = sem("wscaled"), sem("whi_done"), sem("wlo_done"), sem("wr_split")
        var_done, shift_done = sem("var_done"), sem("shift_done")
        stats_done, mv_done, rstd_done, xn_done = sem("stats_done"), sem("mv_done"), sem("rstd_done"), sem("xn_done")
        xt_turned, xt_hi_done, xt_lo_done = sem("xt_turned"), sem("xt_hi_done"), sem("xt_lo_done")
        router_done, z_done, score_done, route_step = sem("router_done"), sem("z_done"), sem("score_done"), sem("route_step")
        gate_done, up_done, silu_done, hmul_done = sem("gate_done"), sem("up_done"), sem("silu_done"), sem("hmul_done")
        hhi_done, hlo_done, down_done, added = sem("hhi_done"), sem("hlo_done"), sem("down_done"), sem("added")
        ones_set, shared_set, power_set = sem("ones_set"), sem("shared_set"), sem("power_set")
        attn_split, consts_cast = sem("attn_split"), sem("consts_cast")
        names = ("low_turned low_hi_done low_lo_done v_projected v_copied g_projected gate_silu gate_ready "
                 "projected slots_done clip_done slots_exp slots_b1 slots_rest slots_b2 slots_b3 rope_parts qk_done "
                 "qk_hi_done qk_lo_done qk_turned qk_t_copied q_t_copied q_spread a_even "
                 "s_done vslot_turned vslot_copied sums_done s_mask_done state_copied logits_done sums_ln sums_guess "
                 "sums_prod sums_inv back_done state_zero "
                 "logit_scaled min_done centred prob_done prob_summed pz_done pinv_done pz_turned p_copied "
                 "a_done a_mask_done o_done o1_done sq_done ss_done o_var_done orstd_done o2_done o3_done o_turned o_copied y_done y_added")
        S = {n: sem(n) for n in names.split()}

        block = ctx.enter_context(nc.Block())

        @block.sync
        def _(sp):
            sp.dma_start(x[:, 0:GT, :], x_d[0]).then_inc(x_loaded[0], 16)
            sp.dma_start(cst[:, :], consts).then_inc(consts_loaded, 16)
            sp.dma_start(wr[:, :], w_router).then_inc(router_loaded, 16)
            sp.dma_start(rbias[:, :], router_bias).then_inc(router_loaded, 16)
            for g in range(1, NG):
                sp.dma_start(x[:, g * GT:(g + 1) * GT, :], x_d[g]).then_inc(x_loaded[g], 16)
            for e in range(1, E):
                if e >= WF:
                    sp.wait_ge(wscaled, e - WF + 2)
                sp.dma_start(wf[:, e % WF, :], w_ffn[e]).then_inc(experts_loaded[e], 16)
            for g in range(NG):
                sp.wait_ge(added, 2 * (SPF + SPF - NG + g + 1))
                sp.dma_start(out_d[g], x[:, g * GT:(g + 1) * GT, :]).then_inc(out_written, 16)
            sp.wait_ge(out_written, 16 * NG)

        @block.scalar
        def _(act):
            act.dma_start(wf[:, 0, :], w_ffn[0]).then_inc(experts_loaded[0], 16)
            for dst, src in ((wqkvg, w_qkvg), (wlow, w_low), (wslots, w_slots), (wo, w_out), (gn, gnorm)):
                act.dma_start(dst[:, :], src).then_inc(attn_loaded, 16)

            def tokens(f):
                for g in range(NG):
                    act.wait_ge(shift_done, NG * f + g + 1)
                    if NG * f + g >= 2:
                        act.wait_ge(xt_turned, NG * f + g - 1)
                    for c in range(GT):
                        i = act.activation(xn[:, g % 2, c, :], x[:, g * GT + c, :], ACT.Identity,
                                           bias=shift[:, g, c:c + 1], scale=rstd[:, g, c:c + 1])
                    i.then_inc(xn_done, 1)
                    act.wait_ge(xt_turned, NG * f + g + 1)
                    if f == 1 and g == 0:
                        act.wait_ge(up_done, IH * SPF)
                    if f == 2 and g == 0:
                        act.wait_ge(S["slots_done"], NC)
                    act.activation(xt_hi[:, g * GW:(g + 1) * GW], xt_ps[g % 2][:, :], ACT.Copy,
                                   scale=XS).then_inc(xt_hi_done, 1)

            def step(f, e, g, first):
                s = SPF * f + NG * e + g
                for ih in range(IH):
                    u = IH * s + ih
                    if not (f == 0 and first and g == 0):
                        act.wait_ge(hmul_done, u - 1)
                    act.wait_ge(gate_done, u + 1)
                    act.activation(gate_s[:, ih, :], gate_ps[ih][:, :], ACT.Silu,
                                   scale=1.0 / (XS * WS)).then_inc(silu_done, 1)
                    act.wait_ge(hmul_done, u + 1)
                    if not (f == 0 and first):
                        act.wait_ge(down_done, 2 * (s - NG) + 2)
                    act.activation(h_hi[:, g, ih, :], h32[:, ih, :], ACT.Copy).then_inc(hhi_done, 1)

            def ffn(f):
                act.wait_ge(z_done, f + 1)
                act.activation(score[:, :, :], score_z[:, :, :], ACT.Sigmoid).then_inc(score_done, 1)
                for g in range(NG):
                    step(f, 0, g, True)
                with act.Fori(1, E) as e:
                    for g in range(NG):
                        step(f, e, g, False)

            def prepare(g):
                act.wait_ge(S["low_turned"], g + 1)
                if g == 0:
                    act.wait_ge(ones_set, 3)
                act.activation(low_hi[0:2 * LOW, g * GW:(g + 1) * GW], low_ps[g % 2], ACT.Copy,
                               scale=1.0 / (XS * WS)).then_inc(S["low_hi_done"], 1)
                act.wait_ge(S["v_projected"], g + 1)
                act.activation(v_all[:, g * GT:(g + 1) * GT, :], v_ps[g % 2][:, :].rearrange("p (c d) -> p c d", d=D), ACT.Copy,
                               scale=1.0 / (XS * WS)).then_inc(S["v_copied"], 1)
                act.wait_ge(S["g_projected"], g + 1)
                act.activation(gate_raw[:, g * GT:(g + 1) * GT, :], g_ps[g % 2][:, :].rearrange("p (c d) -> p c d", d=D), ACT.Silu,
                               scale=1.0 / (XS * WS)).then_inc(S["gate_silu"], 1)

            def front_a(c, p, n):
                act.wait_ge(S["clip_done"], c + 1)
                if n >= 2:
                    act.wait_ge(S["back_done"], c - 1)
                act.activation(slots[:, p, :], clipped[:, p, :], ACT.Exp, scale=1.0 / WS).then_inc(S["slots_exp"], 1)
                act.activation(slot_b1[:, p, :], clipped[:, p, :], ACT.Exp, scale=1.0 / WS).then_inc(S["slots_b1"], 1)

            def front_b(c, p, n):
                act.wait_ge(S["slots_rest"], c + 1)
                act.activation(slot_b2[:, p, :], slot_r[:, :], ACT.Copy).then_inc(S["slots_b2"], 1)

            def front_c(c, p, n):
                act.wait_ge(S["qk_done"], c + 1)
                if n >= 1:
                    act.wait_ge(S["qk_turned"], c)
                act.activation(qk_hi[:, :], qk[:, p, :], ACT.Copy).then_inc(S["qk_hi_done"], 1)

            def front_e(c, p, n):
                act.wait_ge(S["qk_turned"], c + 1)
                if n >= 2:
                    act.wait_ge(S["logits_done"], c - 1)
                    act.wait_ge(S["q_spread"], c - 1)
                act.activation(qk_t[:, p, :, :], qk_t_ps.rearrange("p (a t) -> p a t", a=4), ACT.Copy).then_inc(S["qk_t_copied"], 1)
                act.activation(q_t[:, p, :], q_t_ps, ACT.Copy).then_inc(S["q_t_copied"], 1)

            def mid_d(c, p, n):
                act.wait_ge(S["sums_done"], c + 1)
                if n >= 1:
                    act.wait_ge(S["sums_inv"], c)
                act.activation(slot_ln[:, :], sum_ps[:, :], ACT.Ln).then_inc(S["sums_ln"], 1)

            def mid_e(c, p, n):
                act.wait_ge(S["sums_ln"], c + 1)
                act.activation(slot_i0[:, :], slot_ln[:, :], ACT.Exp, scale=-1.0).then_inc(S["sums_guess"], 1)

            def mid_a(c, p, n):
                act.wait_ge(S["vslot_turned"], c + 1)
                if n >= 2:
                    act.wait_ge(S["a_done"], c - 1)
                act.activation(vslot_t[:, p, :, :], vslot_t_ps.rearrange("p (a b) -> p a b", a=2), ACT.Copy).then_inc(S["vslot_copied"], 1)

            def mid_b(c, p, n):
                if n >= 1:
                    act.wait_ge(S["back_done"], c)
                    if n >= 2:
                        act.wait_ge(S["o_done"], c - 1)
                    for h in range(H):
                        rows, cols = slice(h * DK, (h + 1) * DK), slice(h * M, (h + 1) * M)
                        act.activation(state[rows, p, cols], state_ps[rows, cols], ACT.Copy)
                    for j in range(2):
                        rows = slice(j * M, (j + 1) * M)
                        i = act.activation(state[rows, p, HM:].rearrange("p (a b d) -> p a b d", a=2, d=DK)[:, :, j, :],
                                           state_ps[rows, HM:HM + 4 * DK].rearrange("p (a b d) -> p a b d", a=2, d=DK)[:, :, j, :],
                                           ACT.Copy)
                    i.then_inc(S["state_copied"], 1)

            def mid_c(c, p, n):
                act.wait_ge(S["centred"], c + 1)
                if n >= 1:
                    act.wait_ge(S["pz_done"], c)
                act.activation(prob[:, :], logit_c[:, :], ACT.Exp, scale=-DK ** -0.5).then_inc(S["prob_done"], 1)

            def mid_f(c, p, n):
                act.wait_ge(S["pz_turned"], c + 1)
                if n >= 2:
                    act.wait_ge(S["o_done"], c - 1)
                act.activation(p_t[:, p, :, :], pz_t_ps.rearrange("p (a b) -> p a b", a=2), ACT.Copy, scale=-1.0).then_inc(S["p_copied"], 1)

            def last_a(c, p, n):
                act.wait_ge(S["o_turned"], c + 1)
                if n >= 1:
                    act.wait_ge(S["y_done"], c)
                act.activation(o_t[:, :], o_t_ps, ACT.Copy).then_inc(S["o_copied"], 1)

            def attn_step(i, n):
                front, mid, last, end = stages(i, n)
                if mid:
                    mid_b(*mid)
                if end:
                    last_a(*end)
                if mid:
                    mid_d(*mid)
                if front:
                    front_c(*front)
                if mid:
                    mid_e(*mid)
                if mid:
                    mid_a(*mid)
                if front:
                    front_a(*front)
                if front:
                    front_b(*front)
                if mid:
                    mid_c(*mid)
                if front:
                    front_e(*front)
                if mid:
                    mid_f(*mid)

            tokens(0)
            ffn(0)
            tokens(1)
            for g in range(NG):
                prepare(g)
            act.preload_act_table_set("natural_log_exp_and_others")
            attention(act, attn_step)
            tokens(2)
            ffn(1)

        @block.gpsimd
        def _(pool):
            nc.gpsimd.memset(power[:, :], -0.5).then_inc(power_set, 1)
            nc.gpsimd.memset(low_hi[:, :], 0.0).then_inc(power_set, 1)
            nc.gpsimd.memset(low_lo[:, :], 0.0).then_inc(power_set, 1)
            nc.gpsimd.memset(state[:, :, :], 0.0).then_inc(power_set, 1)
            nc.gpsimd.memset(zero16[:, :], 0.0).then_inc(power_set, 1)
            pool.wait_ge(power_set, 5)

            def root(dst, src, n):
                if n:
                    pool.wait_ge(rstd_done, n)
                nc.gpsimd.tensor_scalar(var_e[:, 0:dst.shape[1]], src, EPS, None, ALU.add).then_inc(var_done, 1)
                pool.wait_ge(var_done, n + 1)
                nc.gpsimd.tensor_tensor(dst, var_e[:, 0:dst.shape[1]], power[:, 0:dst.shape[1]], ALU.pow).then_inc(rstd_done, 1)

            def tokens(f):
                for g in range(NG):
                    pool.wait_ge(mv_done, NG * f + g + 1)
                    if f and g == 0:
                        pool.wait_ge(xn_done, NG * f)
                    root(rstd[:, g, :], mv[:, g, :, 1], NG * f + g)

            tokens(0)

            pool.wait_ge(router_loaded, 32)
            nc.gpsimd.tensor_scalar(wrs[:, :], wr[:, :], WS, None, ALU.mult).then_inc(wscaled, 1)
            pool.wait_ge(wscaled, 1)
            nc.gpsimd.tensor_copy(wr_hi[:, :], wrs[:, :]).then_inc(whi_done, 1)
            pool.wait_ge(whi_done, 1)
            nc.gpsimd.tensor_tensor(wr_lo[:, :], wrs[:, :], wr_hi[:, :], ALU.subtract).then_inc(wr_split, 1)
            for e in range(E):
                pool.wait_ge(experts_loaded[e], 16)
                if e:
                    pool.wait_ge(wlo_done, e)
                nc.gpsimd.tensor_scalar(wsc[:, :], wf[:, e % WF, :], WS, None, ALU.mult).then_inc(wscaled, 1)
                pool.wait_ge(wscaled, e + 2)
                nc.gpsimd.tensor_copy(w_hi[:, e, :], wsc[:, :]).then_inc(whi_done, 1)
                pool.wait_ge(whi_done, e + 2)
                nc.gpsimd.tensor_tensor(w_lo[:, e, :], wsc[:, :], w_hi[:, e, :], ALU.subtract).then_inc(wlo_done, 1)

            def o_root(c, p, n):
                pool.wait_ge(S["o_var_done"], c + 1)
                if n >= 1:
                    pool.wait_ge(S["o3_done"], c)
                nc.gpsimd.tensor_tensor(o_rstd[:, :], o_var[:, :], power[:, 0:H], ALU.pow).then_inc(S["orstd_done"], 1)

            def split(hi, lo, src, scaled, n):
                pool.wait_ge(wlo_done, n)
                nc.gpsimd.tensor_scalar(scaled, src, WS, None, ALU.mult).then_inc(wscaled, 1)
                pool.wait_ge(wscaled, n + 2)
                nc.gpsimd.tensor_copy(hi, scaled).then_inc(whi_done, 1)
                pool.wait_ge(whi_done, n + 2)
                nc.gpsimd.tensor_tensor(lo, scaled, hi, ALU.subtract).then_inc(wlo_done, 1)

            pool.wait_ge(attn_loaded, 80)
            split(wlow_hi[:, :], wlow_lo[:, :], wlow[:, :], wsc[:, 0:2 * LOW], E)
            split(wqkvg_hi[:, :], wqkvg_lo[:, :], wqkvg[:, :], wsc[:, 0:4 * D], E + 1)
            split(wslots_hi[:, :], wslots_lo[:, :], wslots[:, :], wsc[:, 0:2 * HM], E + 2)

            def slot_rests(c, p, n):
                pool.wait_ge(S["slots_b1"], c + 1)
                pool.wait_ge(S["slots_exp"], c + 1)
                if n >= 1:
                    pool.wait_ge(S["slots_b3"], c)
                nc.gpsimd.tensor_tensor(slot_r[:, :], slots[:, p, :], slot_b1[:, p, :], ALU.subtract).then_inc(S["slots_rest"], 1)
                pool.wait_ge(S["slots_b2"], c + 1)
                nc.gpsimd.tensor_tensor(slot_b3[:, p, :], slot_r[:, :], slot_b2[:, p, :], ALU.subtract).then_inc(S["slots_b3"], 1)

            def o_gated(c, p, n):
                pool.wait_ge(S["o1_done"], c + 1)
                if n >= 1:
                    pool.wait_ge(S["o3_done"], c)
                nc.gpsimd.tensor_tensor(o2[:, :], o1[:, :], gates[:, c, :], ALU.mult).then_inc(S["o2_done"], 1)

            def attn_step(i, n):
                front, mid, last, end = stages(i, n)
                if front:
                    slot_rests(*front)
                if last:
                    o_gated(*last)
                if last:
                    o_root(*last)

            tokens(1)
            for g in range(NG):
                pool.wait_ge(S["gate_silu"], g + 1)
                for c in range(g * GT, (g + 1) * GT):
                    i = nc.gpsimd.tensor_tensor(gates[:, c, :], gate_raw[:, c, :], gn[:, :], ALU.mult)
                i.then_inc(S["gate_ready"], 1)
            pool.wait_ge(S["gate_ready"], NG)
            attention(pool, attn_step)
            tokens(2)

        @block.vector
        def _(dve):
            nc.vector.memset(wts[:, :, 0:1], 0.5 / (WS * HS)).then_inc(shared_set, 1)
            dve.wait_ge(consts_loaded, 16)
            nc.vector.tensor_copy(tri16[:, :], tri).then_inc(ones_set, 1)
            nc.vector.tensor_copy(rest16[:, :], rest)
            nc.vector.tensor_copy(ident16[:, :], ident)
            nc.vector.tensor_copy(head16[:, :, :], cst[:, C_HEAD:C_HEAD + H].unsqueeze(2).broadcast_to([P, H, P])).then_inc(ones_set, 1)
            dve.wait_ge(power_set, 5)
            nc.vector.memset(low_hi[2 * LOW:2 * LOW + 1, :], 1.0).then_inc(ones_set, 1)

            def moments(f, g):
                m = NG * f + g
                if f == 0:
                    dve.wait_ge(x_loaded[g], 16)
                elif g == 0:
                    dve.wait_ge(*((added, 2 * SPF) if f == 1 else (S["y_added"], NC)))
                for c in range(GT):
                    i = nc.vector.bn_stats(stats[:, g, c, :], x[:, g * GT + c, :])
                i.then_inc(stats_done, 1)
                dve.wait_ge(stats_done, m + 1)
                for c in range(GT):
                    i = nc.vector.bn_aggr(mv[:, g, c, :], stats[:, g, c, :])
                i.then_inc(mv_done, 1)

            def centre(f, g):
                dve.wait_ge(rstd_done, NG * f + g + 1)
                if f:
                    dve.wait_ge(xn_done, NG * f)
                nc.vector.scalar_tensor_tensor(shift[:, g, :], mv[:, g, :, 0], -1.0, rstd[:, g, :], ALU.mult,
                                               ALU.mult).then_inc(shift_done, 1)

            def low_part(f, g):
                dve.wait_ge(xt_hi_done, NG * f + g + 1)
                nc.vector.scalar_tensor_tensor(xt_lo[:, g * GW:(g + 1) * GW], xt_ps[g % 2][:, :], XS,
                                               xt_hi[:, g * GW:(g + 1) * GW], ALU.mult,
                                               ALU.subtract).then_inc(xt_lo_done, 1)

            def tokens(f):
                moments(f, 0)
                for g in range(NG):
                    if g + 1 < NG:
                        moments(f, g + 1)
                    centre(f, g)
                    if g:
                        low_part(f, g - 1)
                low_part(f, NG - 1)

            routed = [0]

            def chain(ins):
                routed[0] += 1
                ins.then_inc(route_step, 1)
                dve.wait_ge(route_step, routed[0])

            def route(f):
                dve.wait_ge(router_done, f + 1)
                dve.wait_ge(router_loaded, 32)
                nc.vector.scalar_tensor_tensor(score_z[:, :, :], router_ps.rearrange("p (c e) -> p c e", e=ER),
                                               1.0 / (XS * WS), rbias[:, :].unsqueeze(1).broadcast_to([P, NC, ER]), ALU.mult,
                                               ALU.add).then_inc(z_done, 1)
                dve.wait_ge(score_done, f + 1)
                for c in range(NC):
                    i = nc.vector.max(top[:, c, :], score[:, c, :])
                chain(i)
                for c in range(NC):
                    i = nc.vector.max_index(top_at[:, c, :], top[:, c, :], score[:, c, :])
                chain(i)
                nc.vector.tensor_copy(top_af[:, :, :], top_at[:, :, 0:2])
                chain(nc.vector.tensor_tensor(top_sum[:, :], top[:, :, 0], top[:, :, 1], ALU.add))
                chain(nc.vector.reciprocal(top_inv[:, :], top_sum[:, :]))
                chain(nc.vector.scalar_tensor_tensor(share[:, :, :], top[:, :, 0:2], 0.5 / (WS * HS),
                                                     top_inv[:, :].unsqueeze(2).broadcast_to([P, NC, 2]), ALU.mult, ALU.mult))
                for k in range(2):
                    i = nc.vector.tensor_tensor(pick[:, k, :, :], cst[:, C_IOTA:C_IOTA + ER].unsqueeze(1).broadcast_to([P, NC, ER]),
                                                top_af[:, :, k:k + 1].broadcast_to([P, NC, ER]), ALU.is_equal)
                chain(i)
                for k in range(2):
                    i = nc.vector.tensor_tensor(pick[:, k, :, :], pick[:, k, :, :],
                                                share[:, :, k:k + 1].broadcast_to([P, NC, ER]), ALU.mult)
                chain(i)
                chain(nc.vector.tensor_tensor(wts[:, :, 1:E], pick[:, 0, :, :], pick[:, 1, :, :], ALU.add))

            def add_half(f, e, g, j):
                s = SPF * f + NG * e + g
                dve.wait_ge(down_done, 2 * s + j + 1)
                for c in range(2 * j, 2 * j + 2):
                    t = g * GT + c
                    i = nc.vector.scalar_tensor_tensor(x[:, t, :], down_ps[j][:, c % 2 * P:(c % 2 + 1) * P],
                                                       wts[:, t, e:e + 1] if isinstance(e, int) else wts[:, t, bass.ds(e, 1)],
                                                       x[:, t, :], ALU.mult, ALU.add)
                i.then_inc(added, 1)

            def hidden(f, u, ih, first):
                dve.wait_ge(silu_done, u + 1)
                dve.wait_ge(up_done, u + 1)
                if not first:
                    dve.wait_ge(hlo_done, u - 1)
                nc.vector.scalar_tensor_tensor(h32[:, ih, :], up_ps[ih][:, :], HS / (XS * WS), gate_s[:, ih, :],
                                               ALU.mult, ALU.mult).then_inc(hmul_done, 1)

            def rest_of(u, g, ih):
                dve.wait_ge(hhi_done, u + 1)
                nc.vector.tensor_tensor(h_lo[:, g, ih, :], h32[:, ih, :], h_hi[:, g, ih, :],
                                        ALU.subtract).then_inc(hlo_done, 1)

            def step(f, e, g, e2):
                for ih in range(IH):
                    u = IH * (SPF * f + NG * e + g) + ih
                    hidden(f, u, ih, f == 0 and e2 is None and g == 0)
                    if not (e2 is None and g == 0 and ih == 0):
                        rest_of(u - 1, (g - (ih == 0)) % NG, 1 - ih)
                    if not (e2 is None and g < 2):
                        add_half(f, e if g >= 2 else e2, (g - 2) % NG, ih)

            def ffn(f):
                for g in range(NG):
                    step(f, 0, g, None)
                with dve.Fori(1, E) as e:
                    for g in range(NG):
                        step(f, e, g, e - 1)
                rest_of(IH * SPF * (f + 1) - 1, NG - 1, 1)
                for g in (NG - 2, NG - 1):
                    for j in range(2):
                        add_half(f, E - 1, g, j)

            def prepare(g):
                dve.wait_ge(S["low_hi_done"], g + 1)
                nc.vector.scalar_tensor_tensor(low_lo[0:2 * LOW, g * GW:(g + 1) * GW], low_ps[g % 2], 1.0 / (XS * WS),
                                               low_hi[0:2 * LOW, g * GW:(g + 1) * GW], ALU.mult,
                                               ALU.subtract).then_inc(S["low_lo_done"], 1)

            def rope(c, p, n):
                dve.wait_ge(S["projected"], c + 1)
                half = DK // 2
                src = qk_ps[:, 0:2 * D].rearrange("p (a b j) -> p a b j", b=2, j=half)
                dst = rope_s[:, :].rearrange("p (a b j) -> p a b j", b=2, j=half)
                cos = cst[:, bass.ds(C_COS + c * half, half)]
                sin = cst[:, bass.ds(C_SIN + c * half, half)]
                nc.vector.tensor_tensor(rope_c[:, :].rearrange("p (a j) -> p a j", j=half),
                                        qk_ps[:, 0:2 * D].rearrange("p (a j) -> p a j", j=half),
                                        cos.unsqueeze(1).broadcast_to([P, 4 * H, half]), ALU.mult)
                nc.vector.tensor_tensor(dst[:, :, 0, :], src[:, :, 1, :],
                                        sin.unsqueeze(1).broadcast_to([P, 2 * H, half]), ALU.mult)
                nc.vector.tensor_tensor(dst[:, :, 1, :], src[:, :, 0, :],
                                        sin.unsqueeze(1).broadcast_to([P, 2 * H, half]), ALU.mult).then_inc(S["rope_parts"], 1)
                dve.wait_ge(S["rope_parts"], c + 1)
                if n >= 2:
                    dve.wait_ge(S["back_done"], c - 1)
                tc_ = rope_c[:, :].rearrange("p (a b j) -> p a b j", b=2, j=half)
                to = qk[:, p, :].rearrange("p (a b j) -> p a b j", b=2, j=half)
                nc.vector.tensor_tensor(to[:, :, 0, :], tc_[:, :, 0, :], dst[:, :, 0, :], ALU.subtract)
                nc.vector.tensor_tensor(to[:, :, 1, :], tc_[:, :, 1, :], dst[:, :, 1, :], ALU.add).then_inc(S["qk_done"], 1)

            def qk_rest(c, p, n):
                dve.wait_ge(S["qk_hi_done"], c + 1)
                dve.wait_ge(S["qk_done"], c + 1)
                nc.vector.tensor_tensor(qk_lo[:, :], qk[:, p, :], qk_hi[:, :], ALU.subtract).then_inc(S["qk_lo_done"], 1)

            def clip(c, p, n):
                dve.wait_ge(S["slots_done"], c + 1)
                if n >= 2:
                    dve.wait_ge(S["slots_b1"], c - 1)
                nc.vector.tensor_scalar(clipped[:, p, :], slots_ps[:, :], CLAMP * WS, -CLAMP * WS, ALU.min,
                                        ALU.max).then_inc(S["clip_done"], 1)

            def spread_q(c, p, n):
                dve.wait_ge(S["qk_t_copied"], c + 1)
                if n >= 2:
                    dve.wait_ge(S["s_done"], c - 1)
                nc.vector.tensor_tensor(q_heads[:, p, :, :, :], qk_t[:, p, 0:2, :].unsqueeze(2).broadcast_to([P, 2, H, P]),
                                        head16[:, :, :].unsqueeze(1).broadcast_to([P, 2, H, P]),
                                        ALU.mult).then_inc(S["q_spread"], 1)

            def mask_s(c, p, n):
                dve.wait_ge(S["s_done"], c + 1)
                if n >= 2:
                    dve.wait_ge(S["logits_done"], c - 1)
                nc.vector.tensor_tensor(s_masked[:, p, :, :], s_ps[:, :].rearrange("p (h t) -> p h t", h=H),
                                        tri.unsqueeze(1).broadcast_to([P, H, P]), ALU.mult).then_inc(S["s_mask_done"], 1)

            def invert(c, p, n):
                dve.wait_ge(S["sums_guess"], c + 1)
                if n >= 1:
                    dve.wait_ge(S["sums_inv"], c)
                nc.vector.tensor_tensor(slot_zi[:, :], sum_ps[:, :], slot_i0[:, :], ALU.mult).then_inc(S["sums_prod"], 1)
                dve.wait_ge(S["sums_prod"], c + 1)
                nc.vector.scalar_tensor_tensor(slot_inv[:, p, :], slot_zi[:, :], 2.0, slot_i0[:, :], ALU.subtract,
                                               ALU.mult).then_inc(S["sums_inv"], 1)

            def soft_a(c, p, n):
                dve.wait_ge(S["logits_done"], c + 1)
                dve.wait_ge(S["sums_inv"], c + 1)
                nc.vector.tensor_tensor(logit[:, :], logit_ps, slot_inv[:, p, 0:HM], ALU.mult).then_inc(S["logit_scaled"], 1)
                dve.wait_ge(S["logit_scaled"], c + 1)
                lv = logit[:, :].rearrange("p (h m) -> p h m", h=H)
                nc.vector.tensor_reduce(logit_min[:, :], lv, AX_X, ALU.min).then_inc(S["min_done"], 1)
                dve.wait_ge(S["min_done"], c + 1)
                if n >= 1:
                    dve.wait_ge(S["prob_done"], c)
                nc.vector.tensor_tensor(logit_c[:, :].rearrange("p (h m) -> p h m", h=H), lv,
                                        logit_min[:, :].unsqueeze(2).broadcast_to([P, H, M]), ALU.subtract).then_inc(S["centred"], 1)

            def soft_b(c, p, n):
                dve.wait_ge(S["prob_done"], c + 1)
                nc.vector.reduce_sum(prob_sum[:, :], prob[:, :].rearrange("p (h m) -> p h m", h=H), AX_X).then_inc(S["prob_summed"], 1)
                if n >= 1:
                    dve.wait_ge(S["pz_turned"], c)
                nc.vector.tensor_tensor(pz[:, :], prob[:, :], slot_inv[:, p, HM:2 * HM], ALU.mult).then_inc(S["pz_done"], 1)
                dve.wait_ge(S["prob_summed"], c + 1)
                nc.vector.reciprocal(prob_inv[:, p, :], prob_sum[:, :]).then_inc(S["pinv_done"], 1)

            def mask_a(c, p, n):
                dve.wait_ge(S["a_done"], c + 1)
                if n >= 1:
                    dve.wait_ge(S["o_done"], c)
                nc.vector.tensor_tensor(a_masked[:, :, :], c_ps[:, :].rearrange("p (h t) -> p h t", h=H),
                                        tri.unsqueeze(1).broadcast_to([P, H, P]), ALU.mult).then_inc(S["a_mask_done"], 1)

            def norm_a(c, p, n):
                dve.wait_ge(S["o_done"], c + 1)
                dve.wait_ge(S["pinv_done"], c + 1)
                if n >= 1:
                    dve.wait_ge(S["o2_done"], c)
                nc.vector.tensor_tensor(o1[:, :].rearrange("p (h d) -> p h d", h=H), o_ps.rearrange("p (h d) -> p h d", h=H),
                                        prob_inv[:, p, :].unsqueeze(2).broadcast_to([P, H, DK]), ALU.mult).then_inc(S["o1_done"], 1)
                dve.wait_ge(S["o1_done"], c + 1)
                nc.vector.tensor_tensor(o_sq[:, :], o1[:, :], o1[:, :], ALU.mult).then_inc(S["sq_done"], 1)
                dve.wait_ge(S["sq_done"], c + 1)
                nc.vector.reduce_sum(o_ss[:, :], o_sq[:, :].rearrange("p (h d) -> p h d", h=H), AX_X).then_inc(S["ss_done"], 1)
                dve.wait_ge(S["ss_done"], c + 1)
                if n >= 1:
                    dve.wait_ge(S["orstd_done"], c)
                nc.vector.tensor_scalar(o_var[:, :], o_ss[:, :], DK * EPS, None, ALU.add).then_inc(S["o_var_done"], 1)

            def norm_b(c, p, n):
                dve.wait_ge(S["orstd_done"], c + 1)
                dve.wait_ge(S["o2_done"], c + 1)
                if n >= 1:
                    dve.wait_ge(S["o_turned"], c)
                nc.vector.scalar_tensor_tensor(o3[:, :].rearrange("p (h d) -> p h d", h=H), o2[:, :].rearrange("p (h d) -> p h d", h=H),
                                               DK ** 0.5, o_rstd[:, :].unsqueeze(2).broadcast_to([P, H, DK]), ALU.mult,
                                               ALU.mult).then_inc(S["o3_done"], 1)

            def add_y(c, p, n):
                dve.wait_ge(S["y_done"], c + 1)
                nc.vector.tensor_tensor(x[:, c, :], y_ps, x[:, c, :], ALU.add).then_inc(S["y_added"], 1)

            def attn_step(i, n):
                front, mid, last, end = stages(i, n)
                if mid:
                    mask_s(*mid)
                if end:
                    norm_b(*end)
                if front:
                    rope(*front)
                if front:
                    clip(*front)
                if front:
                    qk_rest(*front)
                if last:
                    mask_a(*last)
                if mid:
                    invert(*mid)
                if end:
                    add_y(*end)
                if mid:
                    soft_a(*mid)
                if mid:
                    soft_b(*mid)
                if front:
                    spread_q(*front)
                if last:
                    norm_a(*last)

            tokens(0)
            route(0)
            ffn(0)
            tokens(1)
            for g in range(NG):
                prepare(g)
            attention(dve, attn_step)
            tokens(2)
            route(1)
            ffn(1)

        @block.tensor
        def _(pe):
            mm = nc.tensor.matmul

            def tokens(f):
                for g in range(NG):
                    n = NG * f + g
                    pe.wait_ge(xn_done, n + 1)
                    if f == 2 and g == 0:
                        pe.wait_ge(S["y_added"], NC)
                    if g >= 2:
                        pe.wait_ge(xt_lo_done, n - 1)
                    for c in range(GT):
                        i = nc.tensor.transpose(xt_ps[g % 2][:, c * P:(c + 1) * P], xn[:, g % 2, c, :], ident)
                    i.then_inc(xt_turned, 1)

            def router(f):
                pe.wait_ge(wr_split, 1)
                pe.wait_ge(xt_lo_done, NG * (2 * f + 1))
                for c in range(NC):
                    ts = slice(c * P, (c + 1) * P)
                    dst = router_ps[:, c * ER:(c + 1) * ER]
                    mm(dst, xt_hi[:, ts], wr_hi[:, :], start=True, stop=False)
                    mm(dst, xt_hi[:, ts], wr_lo[:, :], start=False, stop=False)
                    i = mm(dst, xt_lo[:, ts], wr_hi[:, :], start=False, stop=True)
                i.then_inc(router_done, 1)

            def wcols(parts, e, at, n):
                return parts[:, e, at:at + n]

            def down_half(f, e, g, j):
                s = SPF * f + NG * e + g
                pe.wait_ge(hlo_done, 2 * s + 2)
                if not (f == 0 and isinstance(e, int) and e == 0 and g == 0):
                    pe.wait_ge(added, 2 * (s - 1) + j + 1)
                for c in range(2 * j, 2 * j + 2):
                    dst = down_ps[j][:, c % 2 * P:(c % 2 + 1) * P]
                    k = 0
                    for ih in range(IH):
                        at = 2 * I + ih * D
                        for hp, wp in ((h_hi, w_hi), (h_hi, w_lo), (h_lo, w_hi)):
                            i = mm(dst, hp[:, g, ih, c * P:(c + 1) * P], wcols(wp, e, at, D),
                                   start=(k == 0), stop=(k == 3 * IH - 1))
                            k += 1
                i.then_inc(down_done, 1)

            def unit(f, e, g, ih, first):
                u = IH * (SPF * f + NG * e + g) + ih
                if not (f == 0 and first):
                    pe.wait_ge(hmul_done, u - 1)
                ts = slice(g * GW, (g + 1) * GW)
                for at, ps, done in ((ih * P, gate_ps[ih], gate_done), (I + ih * P, up_ps[ih], up_done)):
                    mm(ps[:, :], wcols(w_hi, e, at, P), xt_hi[:, ts], start=True, stop=False)
                    mm(ps[:, :], wcols(w_lo, e, at, P), xt_hi[:, ts], start=False, stop=False)
                    mm(ps[:, :], wcols(w_hi, e, at, P), xt_lo[:, ts], start=False, stop=True).then_inc(done, 1)

            def ffn(f):
                pe.wait_ge(wlo_done, 1)
                for g in range(NG):
                    unit(f, 0, g, 0, g == 0)
                    if g >= 2:
                        down_half(f, 0, g - 2, 1)
                    unit(f, 0, g, 1, g == 0)
                    if g >= 1:
                        down_half(f, 0, g - 1, 0)
                with pe.Fori(1, E) as e:
                    if f == 0:
                        pe.wait_ge(wlo_done, e + 1)
                    for g in range(NG):
                        unit(f, e, g, 0, False)
                        down_half(f, e if g >= 2 else e - 1, (g - 2) % NG, 1)
                        unit(f, e, g, 1, False)
                        down_half(f, e if g >= 1 else e - 1, (g - 1) % NG, 0)
                down_half(f, E - 1, NG - 2, 1)
                for j in range(2):
                    down_half(f, E - 1, NG - 1, j)

            def three(dst, a, b, signal):
                mm(dst, a[0], b[0], start=True, stop=False)
                mm(dst, a[0], b[1], start=False, stop=False)
                mm(dst, a[1], b[0], start=False, stop=True).then_inc(signal, 1)

            def prepare(g):
                ts = slice(g * GW, (g + 1) * GW)
                if g == 0:
                    pe.wait_ge(wlo_done, E + 2)
                    pe.wait_ge(added, 2 * SPF)
                if g >= 2:
                    pe.wait_ge(S["low_lo_done"], g - 1)
                three(low_ps[g % 2], (wlow_hi[:, :], wlow_lo[:, :]), (xt_hi[:, ts], xt_lo[:, ts]), S["low_turned"])
                for ps, at, done, read in ((v_ps[g % 2], 2 * D, "v_projected", "v_copied"), (g_ps[g % 2], 3 * D, "g_projected", "gate_silu")):
                    if g >= 2:
                        pe.wait_ge(S[read], g - 1)
                    for c in range(GT):
                        ts = slice((g * GT + c) * P, (g * GT + c + 1) * P)
                        dst, ws = ps[:, c * D:(c + 1) * D], slice(at, at + D)
                        mm(dst, xt_hi[:, ts], wqkvg_hi[:, ws], start=True, stop=False)
                        mm(dst, xt_hi[:, ts], wqkvg_lo[:, ws], start=False, stop=False)
                        i = mm(dst, xt_lo[:, ts], wqkvg_hi[:, ws], start=False, stop=True)
                    i.then_inc(S[done], 1)

            def project(c, p, n):
                if n >= 1:
                    pe.wait_ge(S["q_t_copied"], c)
                else:
                    pe.wait_ge(S["v_copied"], NG)
                three(qk_ps[:, 0:2 * D], (xt_hi[:, bass.ds(c * P, P)], xt_lo[:, bass.ds(c * P, P)]),
                      (wqkvg_hi[:, 0:2 * D], wqkvg_lo[:, 0:2 * D]), S["projected"])

            def slot_logits(c, p, n):
                if n >= 1:
                    pe.wait_ge(S["clip_done"], c)
                else:
                    pe.wait_ge(wlo_done, E + 3)
                    pe.wait_ge(S["low_lo_done"], NG)
                three(slots_ps[:, :], (low_hi[:, bass.ds(c * P, P)], low_lo[:, bass.ds(c * P, P)]),
                      (wslots_hi[:, :], wslots_lo[:, :]), S["slots_done"])

            def turn_qk(c, p, n):
                pe.wait_ge(S["qk_lo_done"], c + 1)
                nc.tensor.transpose(q_t_ps, qk[:, p, 0:D], ident)
                for a, part in enumerate((qk_hi[:, 0:D], qk_lo[:, 0:D], qk_hi[:, D:2 * D], qk_lo[:, D:2 * D])):
                    i = nc.tensor.transpose(qk_t_ps[:, a * P:(a + 1) * P], part, ident16[:, :])
                i.then_inc(S["qk_turned"], 1)

            def scores(c, p, n):
                pe.wait_ge(S["q_spread"], c + 1)
                if n >= 1:
                    pe.wait_ge(S["logit_scaled"], c)
                else:
                    pe.wait_ge(S["gate_silu"], NG)
                three(s_ps[:, :], (qk_t[:, p, 2, :], qk_t[:, p, 3, :]), (q_heads[:, p, 0, :, :], q_heads[:, p, 1, :, :]), S["s_done"])

            def turn_v(c, p, n):
                pe.wait_ge(S["slots_exp"], c + 1)
                if n >= 1:
                    pe.wait_ge(S["p_copied"], c)
                for a in range(2):
                    i = nc.tensor.transpose(vslot_t_ps[:, a * P:(a + 1) * P], slots[:, p, HM + a * P:HM + (a + 1) * P], ident)
                i.then_inc(S["vslot_turned"], 1)

            def running(c, p, n):
                pe.wait_ge(S["slots_b3"], c + 1)
                if n == 0:
                    pe.wait_ge(S["low_lo_done"], NG)
                for k, part in enumerate((slot_b1, slot_b2, slot_b3)):
                    i = mm(sum_ps[:, :], tri16[:, :], part[:, p, :], start=(n == 0 and k == 0), stop=True, skip_group_check=True)
                i.then_inc(S["sums_done"], 1)

            def logits(c, p, n):
                pe.wait_ge(S["s_mask_done"], c + 1)
                if n >= 1:
                    pe.wait_ge(S["state_copied"], c)
                if n >= 1:
                    mm(logit_ps, q_t[:, p, :], state[:, p, 0:HM], start=True, stop=False, skip_group_check=True)
                for h in range(H):
                    hs = slice(h * M, (h + 1) * M)
                    i = mm(logit_ps[:, hs], s_masked[:, p, h, :], slots[:, p, hs], start=(n == 0), stop=True, skip_group_check=True)
                i.then_inc(S["logits_done"], 1)

            def add_state(c, p, n):
                pe.wait_ge(S["sums_prod"], c + 1)
                for part in (slot_b1, slot_b2, slot_b3):
                    mm(sum_ps[:, :], rest16[:, :], part[:, p, :], start=False, stop=True, skip_group_check=True)
                if n >= 1:
                    pe.wait_ge(S["state_copied"], c)
                mm(state_ps[:, 0:HM], qk[:, p, D:2 * D], slots[:, p, 0:HM], start=False, stop=True, skip_group_check=True)
                for a in range(2):
                    i = mm(state_ps[:, HM + a * 2 * DK:HM + (a + 1) * 2 * DK], slots[:, p, HM + a * P:HM + (a + 1) * P],
                           v_all[:, c, a * 2 * DK:(a + 1) * 2 * DK], start=False, stop=True, skip_group_check=True)
                i.then_inc(S["back_done"], 1)

            def turn_p(c, p, n):
                pe.wait_ge(S["pz_done"], c + 1)
                pe.wait_ge(S["vslot_copied"], c + 1)
                for a in range(2):
                    i = nc.tensor.transpose(pz_t_ps[:, a * P:(a + 1) * P], pz[:, a * P:(a + 1) * P], ident)
                i.then_inc(S["pz_turned"], 1)

            def weights_a(c, p, n):
                pe.wait_ge(S["p_copied"], c + 1)
                pe.wait_ge(S["vslot_copied"], c + 1)
                if n >= 1:
                    pe.wait_ge(S["o1_done"], c)
                for j, done in enumerate(("a_even", "a_done")):
                    rows = slice(j * M, (j + 1) * M)
                    for a in range(2):
                        i = mm(c_ps[:, (2 * a + j) * P:(2 * a + j + 1) * P], vslot_t[rows, p, a, :], p_t[rows, p, a, :], start=True, stop=True)
                    i.then_inc(S[done], 1)
                    if j == 0:
                        pe.wait_ge(S["a_even"], c + 1)

            def outputs(c, p, n):
                pe.wait_ge(S["a_mask_done"], c + 1)
                for h in range(H):
                    hs = slice(h * DK, (h + 1) * DK)
                    if n >= 1 and h % 2 == 0:
                        pair = slice(h * DK, (h + 2) * DK)
                        mm(o_ps[:, pair], p_t[:, p, h // 2, :], state[:, p, HM + h * DK:HM + (h + 2) * DK],
                           start=True, stop=True, skip_group_check=True)
                    i = mm(o_ps[:, hs], a_masked[:, h, :], v_all[:, c, hs], start=(n == 0), stop=True, skip_group_check=True)
                i.then_inc(S["o_done"], 1)

            def turn_o(c, p, n):
                pe.wait_ge(S["o3_done"], c + 1)
                if n >= 1:
                    pe.wait_ge(S["y_added"], c)
                nc.tensor.transpose(o_t_ps, o3[:, :], ident).then_inc(S["o_turned"], 1)

            def out_proj(c, p, n):
                pe.wait_ge(S["o_copied"], c + 1)
                mm(y_ps, o_t[:, :], wo[:, :], start=True, stop=True).then_inc(S["y_done"], 1)

            def attn_step(i, n):
                front, mid, last, end = stages(i, n)
                if mid:
                    scores(*mid)
                if front:
                    project(*front)
                if front:
                    slot_logits(*front)
                if mid:
                    running(*mid)
                if end:
                    turn_o(*end)
                if mid:
                    turn_v(*mid)
                if last:
                    weights_a(*last)
                if mid:
                    logits(*mid)
                if end:
                    out_proj(*end)
                if front:
                    turn_qk(*front)
                if last:
                    outputs(*last)
                if mid:
                    add_state(*mid)
                if mid:
                    turn_p(*mid)

            pe.wait_ge(consts_loaded, 16)
            tokens(0)
            router(0)
            ffn(0)
            tokens(1)
            pe.wait_ge(xt_lo_done, 2 * NG)
            for g in range(NG):
                prepare(g)
            pe.wait_ge(S["low_lo_done"], NG)
            mm(state_ps[:, 0:HM + 4 * DK], zero16[:, 0:P], zero16[:, :], start=True, stop=True, skip_group_check=True)
            attention(pe, attn_step)
            tokens(2)
            router(1)
            ffn(1)


def stages(i, n):
    return [(i - late, (n - late) % 2, n - late) if 0 <= n - late < NC else None
            for late in range(4)]


def attention(eng, step):
    for i in range(4):
        step(i, i)
    with eng.Fori(2, NC // 2) as k:
        step(2 * k, 4)
        step(2 * k + 1, 5)
    for i in range(NC, NC + 3):
        step(i, i)


def kernel(**inputs):
    import numpy as _np
    import concourse.bacc as _bacc
    from concourse import mybir as _mybir
    from concourse.bass_utils import run_bass_kernel_spmd as _run

    a = {k.replace("L0_", ""): _np.asarray(v) for k, v in inputs.items()}
    gate = _np.concatenate([a["ffn_shared_gate"].T[None], a["ffn_gate_w"]])
    up = _np.concatenate([a["ffn_shared_up"].T[None], a["ffn_up_w"]])
    down = _np.concatenate([a["ffn_shared_down"].T[None], a["ffn_down_w"]])
    down = down.reshape(E, IH, P, D).transpose(0, 2, 1, 3).reshape(E, P, IH * D)
    slots = _np.zeros((P, 2 * HM), _np.float32)
    slots[0:LOW, 0:HM] = a["attn_sk_w2"]
    slots[LOW:2 * LOW, HM:] = a["attn_sv_w2"]
    slots[2 * LOW, 0:HM] = a["attn_sk_b2"]
    slots[2 * LOW, HM:] = a["attn_sv_b2"]
    arrays = {
        "x": a["attn_hidden_states"].reshape(T, D),
        "consts": constants(),
        "w_ffn": _np.concatenate([gate, up, down], axis=2),
        "w_router": a["ffn_router_w"].T,
        "router_bias": _np.broadcast_to(a["ffn_routing_bias"], (P, ER)),
        "w_qkvg": _np.concatenate([a["attn_Wq"], a["attn_Wk"], a["attn_Wv"], a["attn_Wg"]], axis=1),
        "w_low": _np.concatenate([a["attn_sk_w1"], a["attn_sv_w1"]], axis=1),
        "w_slots": slots,
        "w_out": a["attn_Wo"],
        "gnorm": _np.broadcast_to(_np.tile(a["attn_gnorm_w"], H), (P, D)),
    }
    nc = _bacc.Bacc("TRN2", target_bir_lowering=False, num_devices=1)
    arrays = {f"in_{k}": _np.ascontiguousarray(v) for k, v in arrays.items()}
    args = [nc.dram_tensor(k, v.shape, _mybir.dt.from_np(v.dtype), kind="ExternalInput").ap() for k, v in arrays.items()]
    args.append(nc.dram_tensor("out_dram", (T, D), _mybir.dt.float32, kind="ExternalOutput").ap())
    macaron_kernel(nc, *args)
    r = _run(nc, [arrays], core_ids=[0])
    return r.results[0]["out_dram"].reshape(1, T, D)
```

```python
from contextlib import ExitStack

import numpy as np
import concourse.bass as bass
from concourse import mybir

ALU = mybir.AluOpType
ACT = mybir.ActivationFunctionType
F32 = mybir.dt.float32
F16 = mybir.dt.float16
BF16 = mybir.dt.bfloat16
U32 = mybir.dt.uint32
AX_X = mybir.AxisListType.X

P = 128
T = 2048
D = 128
NC = T // P
GT = 4
NG = NC // GT
GW = GT * P
ER = 8
E = ER + 1
I = 256
IH = I // P
EW = 3 * I
H = 4
DK = D // H
M = 64
LOW = 16
HM = H * M
EPS = 1e-5
CLAMP = 32.0
XS = 64.0
WS = 64.0
HS = 16.0
WF = 3
BY_DVE = (1, 1, 2)
SPF = NG * E

C_ID = 0
C_TRI = C_ID + P
C_REST = C_TRI + P
C_HEAD = C_REST + P
C_IOTA = C_HEAD + H
C_COS = C_IOTA + ER
C_SIN = C_COS + NC * DK // 2
C_END = C_SIN + NC * DK // 2


def constants():
    half = DK // 2
    inv = np.float32(1.0) / np.float32(10000.0) ** (np.arange(half, dtype=np.float32) / np.float32(half))
    angle = np.arange(T, dtype=np.float32)[:, None] * inv.astype(np.float32)[None, :]
    row = np.arange(P)
    out = np.zeros((P, C_END), np.float32)
    out[:, C_ID:C_ID + P] = np.eye(P)
    out[:, C_TRI:C_TRI + P] = row[:, None] <= row[None, :]
    out[:, C_REST:C_REST + P] = row[:, None] > row[None, :]
    out[:, C_HEAD:C_HEAD + H] = row[:, None] // DK == np.arange(H)[None, :]
    out[:, C_IOTA:C_IOTA + ER] = np.arange(ER)[None, :]
    for at, f in ((C_COS, np.cos), (C_SIN, np.sin)):
        table = (f(angle).astype(np.float32) / np.float32(XS * WS)).reshape(NC, P, half).transpose(1, 0, 2)
        out[:, at:at + NC * half] = table.reshape(P, NC * half)
    return out


def macaron_kernel(nc, x_in, consts, w_ffn, w_router, router_bias, w_qkvg, w_low, w_slots, w_out, gnorm, out):
    x_d = x_in.rearrange("(g c p) d -> g p c d", p=P, c=GT)
    out_d = out.rearrange("(g c p) d -> g p c d", p=P, c=GT)

    with ExitStack() as ctx:
        def sb(name, shape, dt=F32):
            return ctx.enter_context(nc.sbuf_tensor(name, shape, dt))

        def sem(name):
            return ctx.enter_context(nc.semaphore(name))

        x = sb("x", [P, NC, D])
        cst = sb("cst", [P, C_END])
        wf = sb("wf", [P, WF, EW])
        wsc = sb("wsc", [P, EW])
        w_hi = sb("w_hi", [P, E, EW], F16)
        w_lo = sb("w_lo", [P, E, EW], F16)
        wr = sb("wr", [P, ER])
        wr_hi = sb("wr_hi", [P, ER], F16)
        wr_lo = sb("wr_lo", [P, ER], F16)
        rbias = sb("rbias", [P, ER])
        wqkvg = sb("wqkvg", [P, 4 * D])
        wlow = sb("wlow", [P, 2 * LOW])
        wqkvg_hi = sb("wqkvg_hi", [P, 4 * D], F16)
        wqkvg_lo = sb("wqkvg_lo", [P, 4 * D], F16)
        wlow_hi = sb("wlow_hi", [P, 2 * LOW], F16)
        wlow_lo = sb("wlow_lo", [P, 2 * LOW], F16)
        wslots_hi = sb("wslots_hi", [P, 2 * HM], F16)
        wslots_lo = sb("wslots_lo", [P, 2 * HM], F16)
        tri16 = sb("tri16", [P, P], BF16)
        rest16 = sb("rest16", [P, P], BF16)
        head16 = sb("head16", [P, H, P], F16)
        zero16 = sb("zero16", [P, HM + 4 * DK], F16)
        ident16 = sb("ident16", [P, P], F16)
        wslots = sb("wslots", [P, 2 * HM])
        wo = sb("wo", [P, D])
        gn = sb("gn", [P, D])
        stats = sb("stats", [P, NG, GT, 6])
        mv = sb("mv", [P, NG, GT, 2])
        rstd = sb("rstd", [P, NG, GT])
        shift = sb("shift", [P, NG, GT])
        xn = sb("xn", [P, 2, GT, D])
        xt_hi = sb("xt_hi", [P, T], F16)
        xt_lo = sb("xt_lo", [P, T], F16)
        score_z = sb("score_z", [P, NC, ER])
        score = sb("score", [P, NC, ER])
        top = sb("top", [P, NC, 8])
        top_at = sb("top_at", [P, NC, 8], U32)
        top_af = sb("top_af", [P, NC, 2])
        top_sum = sb("top_sum", [P, NC])
        top_inv = sb("top_inv", [P, NC])
        share = sb("share", [P, NC, 2])
        pick = sb("pick", [P, 2, NC, ER])
        wts = sb("wts", [P, NC, E])
        gate_s = sb("gate_s", [P, IH, GW])
        h32 = sb("h32", [P, IH, GW])
        h_hi = sb("h_hi", [P, NG, IH, GW], F16)
        h_lo = sb("h_lo", [P, NG, IH, GW], F16)
        low_hi = sb("low_hi", [P, T], F16)
        low_lo = sb("low_lo", [P, T], F16)
        clipped = sb("clipped", [P, 2, 2 * HM])
        slots = sb("slots", [P, 2, 2 * HM])
        rope_c = sb("rope_c", [P, 2 * D])
        rope_s = sb("rope_s", [P, 2 * D])
        slot_b1 = sb("slot_b1", [P, 2, 2 * HM], BF16)
        slot_r = sb("slot_r", [P, 2 * HM])
        slot_b2 = sb("slot_b2", [P, 2, 2 * HM], BF16)
        slot_b3 = sb("slot_b3", [P, 2, 2 * HM], BF16)
        qk = sb("qk", [P, 2, 2 * D])
        qk_hi = sb("qk_hi", [P, 2 * D], F16)
        qk_lo = sb("qk_lo", [P, 2 * D], F16)
        qk_t = sb("qk_t", [P, 2, 4, P], F16)
        q_t = sb("q_t", [P, 2, P])
        v_all = sb("v_all", [P, NC, D])
        gate_raw = sb("gate_raw", [P, NC, D])
        gates = sb("gates", [P, NC, D])
        state = sb("state", [P, 2, HM + 2 * 2 * DK])
        s_masked = sb("s_masked", [P, 2, H, P])
        slot_inv = sb("slot_inv", [P, 2, 2 * HM])
        slot_ln = sb("slot_ln", [P, 2 * HM])
        slot_i0 = sb("slot_i0", [P, 2 * HM])
        slot_zi = sb("slot_zi", [P, 2 * HM])
        logit = sb("logit", [P, HM])
        logit_min = sb("logit_min", [P, H])
        logit_c = sb("logit_c", [P, HM])
        prob = sb("prob", [P, HM])
        prob_sum = sb("prob_sum", [P, H])
        prob_inv = sb("prob_inv", [P, 2, H])
        pz = sb("pz", [P, HM])
        q_heads = sb("q_heads", [P, 2, 2, H, P], F16)
        p_t = sb("p_t", [P, 2, 2, P])
        vslot_t = sb("vslot_t", [P, 2, 2, P])
        a_masked = sb("a_masked", [P, H, P])
        o1 = sb("o1", [P, D])
        o_sq = sb("o_sq", [P, D])
        o_ss = sb("o_ss", [P, H])
        o_var = sb("o_var", [P, H])
        o_rstd = sb("o_rstd", [P, H])
        var_e = sb("var_e", [P, NC])
        power = sb("power", [P, NC])
        o2 = sb("o2", [P, D])
        o3 = sb("o3", [P, D])
        o_t = sb("o_t", [P, P])

        bank = [ctx.enter_context(nc.psum_tensor(f"bank{b}", [P, 512], F32)) for b in range(8)]
        gate_ps, up_ps, down_ps = [bank[0], bank[1]], [bank[2], bank[3]], [bank[4], bank[5]]
        xt_ps = [bank[6:8], bank[6:8], bank[2:4]]
        router_ps = bank[5][:, 0:NC * ER]
        low_ps, v_ps, g_ps = [b[0:2 * LOW, :] for b in bank[0:2]], bank[2:4], bank[4:6]
        state_ps, sum_ps, qk_ps, slots_ps, s_ps, c_ps, vturn_ps, oturn_ps = bank
        q_t_ps = qk_ps[:, 0:P]
        qk_t_ps = qk_ps[:, P:3 * P].bitcast(F16)
        logit_ps, o_ps = s_ps[:, 0:HM], c_ps[:, 0:P]
        vslot_t_ps, pz_t_ps = vturn_ps[:, 0:HM], vturn_ps[:, HM:2 * HM]
        o_t_ps, y_ps = oturn_ps[:, 0:P], oturn_ps[:, P:2 * P]

        ident, tri, rest = cst[:, C_ID:C_ID + P], cst[:, C_TRI:C_TRI + P], cst[:, C_REST:C_REST + P]

        x_loaded = [sem(f"x_loaded{g}") for g in range(NG)]
        consts_loaded = sem("consts_loaded")
        router_loaded = sem("router_loaded")
        experts_loaded = [sem(f"expert{e}_loaded") for e in range(E)]
        attn_loaded = sem("attn_loaded")
        out_written = sem("out_written")
        wscaled, whi_done, wlo_done, wr_split = sem("wscaled"), sem("whi_done"), sem("wlo_done"), sem("wr_split")
        var_done, shift_done = sem("var_done"), sem("shift_done")
        stats_done, mv_done, rstd_done, xn_done = sem("stats_done"), sem("mv_done"), sem("rstd_done"), sem("xn_done")
        xn_last_done = sem("xn_last_done")
        xt_turned, xt_hi_done, xt_lo_done = sem("xt_turned"), sem("xt_hi_done"), sem("xt_lo_done")
        router_done, z_done, score_done, route_step = sem("router_done"), sem("z_done"), sem("score_done"), sem("route_step")
        gate_done, up_done, silu_done, hmul_done = sem("gate_done"), sem("up_done"), sem("silu_done"), sem("hmul_done")
        hhi_done, hlo_done, down_done, added = sem("hhi_done"), sem("hlo_done"), sem("down_done"), sem("added")
        ones_set, shared_set, power_set = sem("ones_set"), sem("shared_set"), sem("power_set")
        whi0_done, wr_hi_done, wlo0_done = sem("whi0_done"), sem("wr_hi_done"), sem("wlo0_done")
        names = ("low_turned low_hi_done low_lo_done v_projected v_copied g_projected gate_silu gate_ready "
                 "projected slots_done clip_done slots_exp slots_b1 slots_rest slots_b2 slots_b3 rope_parts qk_done "
                 "qk_hi_done qk_lo_done qk_turned qk_t_copied q_t_copied q_spread a_even "
                 "s_done vslot_turned vslot_copied sums_done s_mask_done state_copied logits_done sums_ln sums_guess "
                 "sums_prod sums_inv back_done "
                 "logit_scaled min_done centred prob_done prob_summed pz_done pinv_done pz_turned p_copied "
                 "a_done a_mask_done o_done o1_done sq_done ss_done o_var_done orstd_done o2_done o3_done o_turned o_copied y_done y_added")
        S = {n: sem(n) for n in names.split()}

        block = ctx.enter_context(nc.Block())

        @block.sync
        def _(sp):
            sp.dma_start(x[:, 0:GT, :], x_d[0]).then_inc(x_loaded[0], 16)
            sp.dma_start(cst[:, :], consts).then_inc(consts_loaded, 16)
            sp.dma_start(wr[:, :], w_router).then_inc(router_loaded, 16)
            sp.dma_start(rbias[:, :], router_bias).then_inc(router_loaded, 16)
            for g in range(1, NG):
                sp.dma_start(x[:, g * GT:(g + 1) * GT, :], x_d[g]).then_inc(x_loaded[g], 16)
            for e in range(1, E):
                if e == WF:
                    sp.wait_ge(wlo0_done, 1)
                elif e > WF:
                    sp.wait_ge(wscaled, e - WF)
                sp.dma_start(wf[:, e % WF, :], w_ffn[e]).then_inc(experts_loaded[e], 16)
            for dst, src in ((wqkvg, w_qkvg), (wlow, w_low), (wslots, w_slots), (wo, w_out), (gn, gnorm)):
                sp.dma_start(dst[:, :], src).then_inc(attn_loaded, 16)
            for g in range(NG):
                sp.wait_ge(added, 2 * (SPF + SPF - NG + g + 1))
                sp.dma_start(out_d[g], x[:, g * GT:(g + 1) * GT, :]).then_inc(out_written, 16)
            sp.wait_ge(out_written, 16 * NG)

        @block.scalar
        def _(act):
            act.dma_start(wf[:, 0, :], w_ffn[0]).then_inc(experts_loaded[0], 16)

            def split_first():
                act.wait_ge(router_loaded, 32)
                act.activation(wr_hi[:, :], wr[:, :], ACT.Copy, scale=WS).then_inc(wr_hi_done, 1)
                act.wait_ge(experts_loaded[0], 16)
                act.activation(w_hi[:, 0, :], wf[:, 0, :], ACT.Copy, scale=WS).then_inc(whi0_done, 1)

            def apply(k, g):
                act.wait_ge(shift_done, NG * k + g + 1)
                if NG * k + g >= 2:
                    act.wait_ge(xt_turned, NG * k + g - 1)
                for c in range(GT - BY_DVE[k]):
                    i = act.activation(xn[:, g % 2, c, :], x[:, g * GT + c, :], ACT.Identity,
                                       bias=shift[:, g, c:c + 1], scale=rstd[:, g, c:c + 1])
                i.then_inc(xn_done, 1)

            def high(k, g):
                act.wait_ge(xt_turned, NG * k + g + 1)
                if k == 1:
                    act.wait_ge(up_done, IH * (NG * (E - 1) + g + 1))
                if k == 2 and g == 0:
                    act.wait_ge(S["slots_done"], NC)
                    act.wait_ge(S["projected"], NC)
                act.activation(xt_hi[:, g * GW:(g + 1) * GW], xt_ps[k][g % 2][:, :], ACT.Copy,
                               scale=XS).then_inc(xt_hi_done, 1)

            def step(f, e, g, first):
                s = SPF * f + NG * e + g
                for ih in range(IH):
                    u = IH * s + ih
                    if not (f == 0 and first and g == 0):
                        act.wait_ge(hmul_done, u - 1)
                    act.wait_ge(gate_done, u + 1)
                    act.activation(gate_s[:, ih, :], gate_ps[ih][:, :], ACT.Silu,
                                   scale=1.0 / (XS * WS)).then_inc(silu_done, 1)
                    act.wait_ge(hmul_done, u + 1)
                    if not (f == 0 and first):
                        act.wait_ge(down_done, 2 * (s - NG) + 2)
                    act.activation(h_hi[:, g, ih, :], h32[:, ih, :], ACT.Copy).then_inc(hhi_done, 1)

            def scores(f):
                act.wait_ge(z_done, f + 1)
                act.activation(score[:, :, :], score_z[:, :, :], ACT.Sigmoid).then_inc(score_done, 1)
                act.preload_act_table(ACT.Silu)

            def ffn(f):
                for g in range(NG):
                    step(f, 0, g, True)
                with act.Fori(1, E - 1 if f == 0 else E) as e:
                    for g in range(NG):
                        step(f, e, g, False)
                if f == 0:
                    for g in range(NG):
                        step(f, E - 1, g, False)

            def prepare(g):
                act.wait_ge(S["low_turned"], g + 1)
                if g == 0:
                    act.wait_ge(ones_set, 2)
                act.activation(low_hi[0:2 * LOW, g * GW:(g + 1) * GW], low_ps[g % 2], ACT.Copy,
                               scale=1.0 / (XS * WS)).then_inc(S["low_hi_done"], 1)
                act.wait_ge(S["v_projected"], g + 1)
                act.activation(v_all[:, g * GT:(g + 1) * GT, :], v_ps[g % 2][:, :].rearrange("p (c d) -> p c d", d=D), ACT.Copy,
                               scale=1.0 / (XS * WS)).then_inc(S["v_copied"], 1)
                act.wait_ge(S["g_projected"], g + 1)
                act.activation(gate_raw[:, g * GT:(g + 1) * GT, :], g_ps[g % 2][:, :].rearrange("p (c d) -> p c d", d=D), ACT.Silu,
                               scale=1.0 / (XS * WS)).then_inc(S["gate_silu"], 1)

            def slots_exponent(c, p, n):
                act.wait_ge(S["clip_done"], c + 1)
                if n >= 2:
                    act.wait_ge(S["back_done"], c - 1)
                act.activation(slots[:, p, :], clipped[:, p, :], ACT.Exp, scale=1.0 / WS).then_inc(S["slots_exp"], 1)

            def slots_high(c, p, n):
                act.wait_ge(S["clip_done"], c + 1)
                if n >= 2:
                    act.wait_ge(S["back_done"], c - 1)
                act.activation(slot_b1[:, p, :], clipped[:, p, :], ACT.Exp, scale=1.0 / WS).then_inc(S["slots_b1"], 1)

            def slots_middle(c, p, n):
                act.wait_ge(S["slots_rest"], c + 1)
                act.activation(slot_b2[:, p, :], slot_r[:, :], ACT.Copy).then_inc(S["slots_b2"], 1)

            def qk_high(c, p, n):
                act.wait_ge(S["qk_done"], c + 1)
                if n >= 1:
                    act.wait_ge(S["qk_turned"], c)
                act.activation(qk_hi[:, :], qk[:, p, :], ACT.Copy).then_inc(S["qk_hi_done"], 1)

            def copy_qk_parts(c, p, n):
                act.wait_ge(S["qk_turned"], c + 1)
                if n >= 2:
                    act.wait_ge(S["logits_done"], c - 1)
                    act.wait_ge(S["q_spread"], c - 1)
                act.activation(qk_t[:, p, :, :], qk_t_ps.rearrange("p (a t) -> p a t", a=4), ACT.Copy).then_inc(S["qk_t_copied"], 1)

            def copy_q(c, p, n):
                act.activation(q_t[:, p, :], q_t_ps, ACT.Copy).then_inc(S["q_t_copied"], 1)

            def sums_log(c, p, n):
                act.wait_ge(S["sums_done"], c + 1)
                if n >= 1:
                    act.wait_ge(S["sums_inv"], c)
                act.activation(slot_ln[:, :], sum_ps[:, :], ACT.Ln).then_inc(S["sums_ln"], 1)

            def sums_first_inverse(c, p, n):
                act.wait_ge(S["sums_ln"], c + 1)
                act.activation(slot_i0[:, :], slot_ln[:, :], ACT.Exp, scale=-1.0).then_inc(S["sums_guess"], 1)

            def copy_value_slots(c, p, n):
                act.wait_ge(S["vslot_turned"], c + 1)
                if n >= 2:
                    act.wait_ge(S["a_done"], c - 1)
                act.activation(vslot_t[:, p, :, :], vslot_t_ps.rearrange("p (a b) -> p a b", a=2), ACT.Copy).then_inc(S["vslot_copied"], 1)

            def copy_state(c, p, n):
                if n >= 1:
                    act.wait_ge(S["back_done"], c)
                    if n >= 2:
                        act.wait_ge(S["o_done"], c - 1)
                    for h in range(H):
                        rows, cols = slice(h * DK, (h + 1) * DK), slice(h * M, (h + 1) * M)
                        act.activation(state[rows, p, cols], state_ps[rows, cols], ACT.Copy)
                    for j in range(2):
                        rows = slice(j * M, (j + 1) * M)
                        i = act.activation(state[rows, p, HM:].rearrange("p (a b d) -> p a b d", a=2, d=DK)[:, :, j, :],
                                           state_ps[rows, HM:HM + 4 * DK].rearrange("p (a b d) -> p a b d", a=2, d=DK)[:, :, j, :],
                                           ACT.Copy)
                    i.then_inc(S["state_copied"], 1)

            def soft_exp(c, p, n):
                act.wait_ge(S["centred"], c + 1)
                if n >= 1:
                    act.wait_ge(S["pz_done"], c)
                    act.wait_ge(S["prob_summed"], c)
                act.activation(prob[:, :], logit_c[:, :], ACT.Exp, scale=-DK ** -0.5).then_inc(S["prob_done"], 1)

            def copy_p(c, p, n):
                act.wait_ge(S["pz_turned"], c + 1)
                if n >= 2:
                    act.wait_ge(S["o_done"], c - 1)
                act.activation(p_t[:, p, :, :], pz_t_ps.rearrange("p (a b) -> p a b", a=2), ACT.Copy, scale=-1.0).then_inc(S["p_copied"], 1)

            def o_square(c, p, n):
                act.wait_ge(S["o1_done"], c + 1)
                if n >= 1:
                    act.wait_ge(S["ss_done"], c)
                act.activation(o_sq[:, :], o1[:, :], ACT.Square).then_inc(S["sq_done"], 1)

            def copy_o(c, p, n):
                act.wait_ge(S["o_turned"], c + 1)
                if n >= 1:
                    act.wait_ge(S["y_done"], c)
                act.activation(o_t[:, :], o_t_ps, ACT.Copy).then_inc(S["o_copied"], 1)

            def attn_step(i, n):
                front, mid, last, end = stages(i, n)
                if mid:
                    copy_state(*mid)
                if mid:
                    sums_log(*mid)
                if mid:
                    copy_value_slots(*mid)
                if mid:
                    sums_first_inverse(*mid)
                if end:
                    copy_o(*end)
                if front:
                    qk_high(*front)
                if front:
                    slots_high(*front)
                if front:
                    slots_exponent(*front)
                if front:
                    copy_qk_parts(*front)
                if front:
                    slots_middle(*front)
                if mid:
                    soft_exp(*mid)
                if last:
                    o_square(*last)
                if front:
                    copy_q(*front)
                if mid:
                    copy_p(*mid)

            def before(i):
                if i == NC + 1:
                    act.preload_act_table(ACT.Sigmoid)
                if i == NC + 2:
                    apply(2, 0)

            act.preload_act_table(ACT.Sigmoid)
            apply(0, 0)
            split_first()
            apply(0, 1)
            high(0, 0)
            apply(0, 2)
            high(0, 1)
            apply(0, 3)
            high(0, 2)
            high(0, 3)
            scores(0)
            ffn(0)
            apply(1, 0)
            apply(1, 1)
            high(1, 0)
            apply(1, 2)
            high(1, 1)
            apply(1, 3)
            high(1, 2)
            prepare(0)
            high(1, 3)
            for g in range(1, NG):
                prepare(g)
            act.preload_act_table_set("natural_log_exp_and_others")
            attention(act, attn_step, before)
            apply(2, 1)
            high(2, 0)
            apply(2, 2)
            high(2, 1)
            apply(2, 3)
            high(2, 2)
            high(2, 3)
            scores(1)
            ffn(1)

        @block.gpsimd
        def _(pool):
            nc.gpsimd.memset(power[:, :], -0.5).then_inc(power_set, 1)
            pool.wait_ge(power_set, 1)

            def root(dst, src, n):
                if n:
                    pool.wait_ge(rstd_done, n)
                nc.gpsimd.tensor_scalar(var_e[:, 0:dst.shape[1]], src, EPS, None, ALU.add).then_inc(var_done, 1)
                pool.wait_ge(var_done, n + 1)
                nc.gpsimd.tensor_tensor(dst, var_e[:, 0:dst.shape[1]], power[:, 0:dst.shape[1]], ALU.pow).then_inc(rstd_done, 1)

            def tokens(f, first, end):
                for g in range(first, end):
                    pool.wait_ge(mv_done, NG * f + g + 1)
                    if f and g == 0:
                        pool.wait_ge(xn_done, NG * f)
                    root(rstd[:, g, :], mv[:, g, :, 1], NG * f + g)

            tokens(0, 0, NG)

            for e in range(1, E):
                pool.wait_ge(experts_loaded[e], 16)
                if e > 1:
                    pool.wait_ge(wlo_done, e - 1)
                nc.gpsimd.tensor_scalar(wsc[:, :], wf[:, e % WF, :], WS, None, ALU.mult).then_inc(wscaled, 1)
                pool.wait_ge(wscaled, e)
                nc.gpsimd.tensor_copy(w_hi[:, e, :], wsc[:, :]).then_inc(whi_done, 1)
                pool.wait_ge(whi_done, e)
                nc.gpsimd.tensor_tensor(w_lo[:, e, :], wsc[:, :], w_hi[:, e, :], ALU.subtract).then_inc(wlo_done, 1)

            def root_o(c, p, n):
                pool.wait_ge(S["o_var_done"], c + 1)
                if n >= 1:
                    pool.wait_ge(S["o3_done"], c)
                nc.gpsimd.tensor_tensor(o_rstd[:, :], o_var[:, :], power[:, 0:H], ALU.pow).then_inc(S["orstd_done"], 1)

            def split(hi, lo, src, scaled, n):
                pool.wait_ge(wlo_done, n)
                nc.gpsimd.tensor_scalar(scaled, src, WS, None, ALU.mult).then_inc(wscaled, 1)
                pool.wait_ge(wscaled, n + 1)
                nc.gpsimd.tensor_copy(hi, scaled).then_inc(whi_done, 1)
                pool.wait_ge(whi_done, n + 1)
                nc.gpsimd.tensor_tensor(lo, scaled, hi, ALU.subtract).then_inc(wlo_done, 1)

            pool.wait_ge(attn_loaded, 80)
            split(wlow_hi[:, :], wlow_lo[:, :], wlow[:, :], wsc[:, 0:2 * LOW], E - 1)
            split(wqkvg_hi[:, :], wqkvg_lo[:, :], wqkvg[:, :], wsc[:, 0:4 * D], E)
            split(wslots_hi[:, :], wslots_lo[:, :], wslots[:, :], wsc[:, 0:2 * HM], E + 1)

            for zeros in (low_hi[:, :], low_lo[:, :], state[:, :, :], zero16[:, :]):
                nc.gpsimd.memset(zeros, 0.0)
            pool.wait_ge(consts_loaded, 16)
            nc.gpsimd.tensor_copy(tri16[:, :], tri)
            nc.gpsimd.tensor_copy(rest16[:, :], rest)
            nc.gpsimd.tensor_copy(ident16[:, :], ident)
            nc.gpsimd.tensor_copy(head16[:, :, :], cst[:, C_HEAD:C_HEAD + H].unsqueeze(2).broadcast_to([P, H, P])).then_inc(ones_set, 1)
            pool.wait_ge(ones_set, 1)
            nc.gpsimd.memset(low_hi[2 * LOW:2 * LOW + 1, :], 1.0).then_inc(ones_set, 1)
            pool.wait_ge(ones_set, 2)

            def slots_rest(c, p, n):
                pool.wait_ge(S["slots_b1"], c + 1)
                pool.wait_ge(S["slots_exp"], c + 1)
                if n >= 1:
                    pool.wait_ge(S["slots_b3"], c)
                nc.gpsimd.tensor_tensor(slot_r[:, :], slots[:, p, :], slot_b1[:, p, :], ALU.subtract).then_inc(S["slots_rest"], 1)

            def slots_low(c, p, n):
                pool.wait_ge(S["slots_b2"], c + 1)
                nc.gpsimd.tensor_tensor(slot_b3[:, p, :], slot_r[:, :], slot_b2[:, p, :], ALU.subtract).then_inc(S["slots_b3"], 1)

            def rope_add(c, p, n):
                half = DK // 2
                dst = rope_s[:, :].rearrange("p (a b j) -> p a b j", b=2, j=half)
                pool.wait_ge(S["rope_parts"], c + 1)
                if n >= 2:
                    pool.wait_ge(S["back_done"], c - 1)
                tc_ = rope_c[:, :].rearrange("p (a b j) -> p a b j", b=2, j=half)
                to = qk[:, p, :].rearrange("p (a b j) -> p a b j", b=2, j=half)
                nc.gpsimd.tensor_tensor(to[:, :, 0, :], tc_[:, :, 0, :], dst[:, :, 0, :], ALU.subtract)
                nc.gpsimd.tensor_tensor(to[:, :, 1, :], tc_[:, :, 1, :], dst[:, :, 1, :], ALU.add).then_inc(S["qk_done"], 1)

            def qk_low(c, p, n):
                pool.wait_ge(S["qk_hi_done"], c + 1)
                pool.wait_ge(S["qk_done"], c + 1)
                nc.gpsimd.tensor_tensor(qk_lo[:, :], qk[:, p, :], qk_hi[:, :], ALU.subtract).then_inc(S["qk_lo_done"], 1)

            def gate_o(c, p, n):
                pool.wait_ge(S["o1_done"], c + 1)
                if n >= 1:
                    pool.wait_ge(S["o3_done"], c)
                nc.gpsimd.tensor_tensor(o2[:, :], o1[:, :], gates[:, c, :], ALU.mult).then_inc(S["o2_done"], 1)

            def attn_step(i, n):
                front, mid, last, end = stages(i, n)
                if front:
                    rope_add(*front)
                if front:
                    qk_low(*front)
                if front:
                    slots_rest(*front)
                if front:
                    slots_low(*front)
                if last:
                    gate_o(*last)
                if last:
                    root_o(*last)

            def before(i):
                if i == NC + 1:
                    tokens(2, 0, 2)

            tokens(1, 0, NG)
            for g in range(NG):
                pool.wait_ge(S["gate_silu"], g + 1)
                for c in range(g * GT, (g + 1) * GT):
                    i = nc.gpsimd.tensor_tensor(gates[:, c, :], gate_raw[:, c, :], gn[:, :], ALU.mult)
                i.then_inc(S["gate_ready"], 1)
            pool.wait_ge(S["gate_ready"], NG)
            attention(pool, attn_step, before)
            tokens(2, 2, NG)

        @block.vector
        def _(dve):
            nc.vector.memset(wts[:, :, 0:1], 0.5 / (WS * HS)).then_inc(shared_set, 1)

            def split_first():
                dve.wait_ge(wr_hi_done, 1)
                nc.vector.scalar_tensor_tensor(wr_lo[:, :], wr[:, :], WS, wr_hi[:, :], ALU.mult, ALU.subtract).then_inc(wr_split, 1)
                dve.wait_ge(whi0_done, 1)
                nc.vector.scalar_tensor_tensor(w_lo[:, 0, :], wf[:, 0, :], WS, w_hi[:, 0, :], ALU.mult, ALU.subtract).then_inc(wlo0_done, 1)

            def moments(f, g):
                m = NG * f + g
                if f == 0:
                    dve.wait_ge(x_loaded[g], 16)
                elif f == 1:
                    dve.wait_ge(added, 2 * (NG * (E - 1) + g + 1))
                else:
                    dve.wait_ge(S["y_added"], GT * (g + 1))
                for c in range(GT):
                    i = nc.vector.bn_stats(stats[:, g, c, :], x[:, g * GT + c, :])
                i.then_inc(stats_done, 1)
                dve.wait_ge(stats_done, m + 1)
                for c in range(GT):
                    i = nc.vector.bn_aggr(mv[:, g, c, :], stats[:, g, c, :])
                i.then_inc(mv_done, 1)

            def centre(f, g):
                dve.wait_ge(rstd_done, NG * f + g + 1)
                if f:
                    dve.wait_ge(xn_done, NG * f)
                nc.vector.scalar_tensor_tensor(shift[:, g, :], mv[:, g, :, 0], -1.0, rstd[:, g, :], ALU.mult,
                                               ALU.mult).then_inc(shift_done, 1)
                if NG * f + g >= 2:
                    dve.wait_ge(xt_turned, NG * f + g - 1)
                for c in range(GT - BY_DVE[f], GT):
                    i = nc.vector.tensor_scalar(xn[:, g % 2, c, :], x[:, g * GT + c, :], mv[:, g, c, 0:1], rstd[:, g, c:c + 1],
                                                ALU.subtract, ALU.mult)
                i.then_inc(xn_last_done, 1)

            def low_part(f, g):
                dve.wait_ge(xt_hi_done, NG * f + g + 1)
                nc.vector.scalar_tensor_tensor(xt_lo[:, g * GW:(g + 1) * GW], xt_ps[f][g % 2][:, :], XS,
                                               xt_hi[:, g * GW:(g + 1) * GW], ALU.mult,
                                               ALU.subtract).then_inc(xt_lo_done, 1)

            def route_z(f):
                dve.wait_ge(router_done, NG * (f + 1))
                dve.wait_ge(router_loaded, 32)
                nc.vector.scalar_tensor_tensor(score_z[:, :, :], router_ps.rearrange("p (c e) -> p c e", e=ER),
                                               1.0 / (XS * WS), rbias[:, :].unsqueeze(1).broadcast_to([P, NC, ER]), ALU.mult,
                                               ALU.add).then_inc(z_done, 1)

            def routed(f, n):
                dve.wait_ge(route_step, 8 * f + n)

            def route_best(f):
                dve.wait_ge(score_done, f + 1)
                for c in range(NC):
                    i = nc.vector.max(top[:, c, :], score[:, c, :])
                i.then_inc(route_step, 1)

            def route_which(f):
                routed(f, 1)
                for c in range(NC):
                    i = nc.vector.max_index(top_at[:, c, :], top[:, c, :], score[:, c, :])
                i.then_inc(route_step, 1)

            def route_sum(f):
                routed(f, 2)
                nc.vector.tensor_copy(top_af[:, :, :], top_at[:, :, 0:2])
                nc.vector.tensor_tensor(top_sum[:, :], top[:, :, 0], top[:, :, 1], ALU.add).then_inc(route_step, 1)

            def route_inverse(f):
                routed(f, 3)
                nc.vector.reciprocal(top_inv[:, :], top_sum[:, :]).then_inc(route_step, 1)

            def route_share(f):
                routed(f, 4)
                nc.vector.scalar_tensor_tensor(share[:, :, :], top[:, :, 0:2], 0.5 / (WS * HS),
                                               top_inv[:, :].unsqueeze(2).broadcast_to([P, NC, 2]), ALU.mult,
                                               ALU.mult).then_inc(route_step, 1)

            def route_pick(f):
                routed(f, 5)
                for k in range(2):
                    i = nc.vector.tensor_tensor(pick[:, k, :, :], cst[:, C_IOTA:C_IOTA + ER].unsqueeze(1).broadcast_to([P, NC, ER]),
                                                top_af[:, :, k:k + 1].broadcast_to([P, NC, ER]), ALU.is_equal)
                i.then_inc(route_step, 1)

            def route_weigh(f):
                routed(f, 6)
                for k in range(2):
                    i = nc.vector.tensor_tensor(pick[:, k, :, :], pick[:, k, :, :],
                                                share[:, :, k:k + 1].broadcast_to([P, NC, ER]), ALU.mult)
                i.then_inc(route_step, 1)

            def route_weights(f):
                routed(f, 7)
                nc.vector.tensor_tensor(wts[:, :, 1:E], pick[:, 0, :, :], pick[:, 1, :, :], ALU.add).then_inc(route_step, 1)

            def add_half(f, e, g, j):
                s = SPF * f + NG * e + g
                dve.wait_ge(down_done, 2 * s + j + 1)
                for c in range(2 * j, 2 * j + 2):
                    t = g * GT + c
                    i = nc.vector.scalar_tensor_tensor(x[:, t, :], down_ps[j][:, c % 2 * P:(c % 2 + 1) * P],
                                                       wts[:, t, e:e + 1] if isinstance(e, int) else wts[:, t, bass.ds(e, 1)],
                                                       x[:, t, :], ALU.mult, ALU.add)
                i.then_inc(added, 1)

            def hidden(f, u, ih, first):
                dve.wait_ge(silu_done, u + 1)
                dve.wait_ge(up_done, u + 1)
                if not first:
                    dve.wait_ge(hlo_done, u - 1)
                nc.vector.scalar_tensor_tensor(h32[:, ih, :], up_ps[ih][:, :], HS / (XS * WS), gate_s[:, ih, :],
                                               ALU.mult, ALU.mult).then_inc(hmul_done, 1)

            def rest_of(u, g, ih):
                dve.wait_ge(hhi_done, u + 1)
                nc.vector.tensor_tensor(h_lo[:, g, ih, :], h32[:, ih, :], h_hi[:, g, ih, :],
                                        ALU.subtract).then_inc(hlo_done, 1)

            def step(f, e, g, e2, extras=(None, None)):
                for ih in range(IH):
                    u = IH * (SPF * f + NG * e + g) + ih
                    if not (e2 is None and g < 2):
                        add_half(f, e if g >= 2 else e2, (g - 2) % NG, ih)
                    hidden(f, u, ih, f == 0 and e2 is None and g == 0)
                    if not (e2 is None and g == 0 and ih == 0):
                        rest_of(u - 1, (g - (ih == 0)) % NG, 1 - ih)
                    if extras[ih]:
                        extras[ih](f)

            def ffn(f):
                step(f, 0, 0, None, (route_best, None))
                step(f, 0, 1, None, (route_which, route_sum))
                step(f, 0, 2, None, (route_inverse, route_share))
                step(f, 0, 3, None, (route_pick, route_weigh))
                route_weights(f)
                routed(f, 8)
                with dve.Fori(1, E - 1 if f == 0 else E) as e:
                    for g in range(NG):
                        step(f, e, g, e - 1)
                if f == 0:
                    for g in range(NG):
                        step(f, E - 1, g, E - 2)
                        if g == 2:
                            moments(1, 0)
                    centre(1, 0)
                    moments(1, 1)
                rest_of(IH * SPF * (f + 1) - 1, NG - 1, 1)
                for g in (NG - 2, NG - 1):
                    for j in range(2):
                        add_half(f, E - 1, g, j)
                    if f == 0:
                        moments(1, g)
                        centre(1, g - 1)

            def prepare(g):
                dve.wait_ge(S["low_hi_done"], g + 1)
                nc.vector.scalar_tensor_tensor(low_lo[0:2 * LOW, g * GW:(g + 1) * GW], low_ps[g % 2], 1.0 / (XS * WS),
                                               low_hi[0:2 * LOW, g * GW:(g + 1) * GW], ALU.mult,
                                               ALU.subtract).then_inc(S["low_lo_done"], 1)

            def rope_multiply(c, p, n):
                if n >= 1:
                    dve.wait_ge(S["qk_done"], c)
                dve.wait_ge(S["projected"], c + 1)
                half = DK // 2
                src = qk_ps[:, 0:2 * D].rearrange("p (a b j) -> p a b j", b=2, j=half)
                dst = rope_s[:, :].rearrange("p (a b j) -> p a b j", b=2, j=half)
                cos = cst[:, bass.ds(C_COS + c * half, half)]
                sin = cst[:, bass.ds(C_SIN + c * half, half)]
                nc.vector.tensor_tensor(rope_c[:, :].rearrange("p (a j) -> p a j", j=half),
                                        qk_ps[:, 0:2 * D].rearrange("p (a j) -> p a j", j=half),
                                        cos.unsqueeze(1).broadcast_to([P, 4 * H, half]), ALU.mult)
                nc.vector.tensor_tensor(dst[:, :, 0, :], src[:, :, 1, :],
                                        sin.unsqueeze(1).broadcast_to([P, 2 * H, half]), ALU.mult)
                nc.vector.tensor_tensor(dst[:, :, 1, :], src[:, :, 0, :],
                                        sin.unsqueeze(1).broadcast_to([P, 2 * H, half]), ALU.mult).then_inc(S["rope_parts"], 1)

            def clip_slots(c, p, n):
                dve.wait_ge(S["slots_done"], c + 1)
                if n >= 2:
                    dve.wait_ge(S["slots_b1"], c - 1)
                nc.vector.tensor_scalar(clipped[:, p, :], slots_ps[:, :], CLAMP * WS, -CLAMP * WS, ALU.min,
                                        ALU.max).then_inc(S["clip_done"], 1)

            def spread_q(c, p, n):
                dve.wait_ge(S["qk_t_copied"], c + 1)
                if n >= 2:
                    dve.wait_ge(S["s_done"], c - 1)
                nc.vector.tensor_tensor(q_heads[:, p, :, :, :], qk_t[:, p, 0:2, :].unsqueeze(2).broadcast_to([P, 2, H, P]),
                                        head16[:, :, :].unsqueeze(1).broadcast_to([P, 2, H, P]),
                                        ALU.mult).then_inc(S["q_spread"], 1)

            def mask_s(c, p, n):
                dve.wait_ge(S["s_done"], c + 1)
                if n >= 2:
                    dve.wait_ge(S["logits_done"], c - 1)
                nc.vector.tensor_tensor(s_masked[:, p, :, :], s_ps[:, :].rearrange("p (h t) -> p h t", h=H),
                                        tri.unsqueeze(1).broadcast_to([P, H, P]), ALU.mult).then_inc(S["s_mask_done"], 1)

            def sums_product(c, p, n):
                dve.wait_ge(S["sums_guess"], c + 1)
                if n >= 1:
                    dve.wait_ge(S["sums_inv"], c)
                nc.vector.tensor_tensor(slot_zi[:, :], sum_ps[:, :], slot_i0[:, :], ALU.mult).then_inc(S["sums_prod"], 1)

            def sums_inverse(c, p, n):
                dve.wait_ge(S["sums_prod"], c + 1)
                nc.vector.scalar_tensor_tensor(slot_inv[:, p, :], slot_zi[:, :], 2.0, slot_i0[:, :], ALU.subtract,
                                               ALU.mult).then_inc(S["sums_inv"], 1)

            def soft_scale(c, p, n):
                dve.wait_ge(S["logits_done"], c + 1)
                dve.wait_ge(S["sums_inv"], c + 1)
                nc.vector.tensor_tensor(logit[:, :], logit_ps, slot_inv[:, p, 0:HM], ALU.mult).then_inc(S["logit_scaled"], 1)

            def soft_min(c, p, n):
                dve.wait_ge(S["logit_scaled"], c + 1)
                lv = logit[:, :].rearrange("p (h m) -> p h m", h=H)
                nc.vector.tensor_reduce(logit_min[:, :], lv, AX_X, ALU.min).then_inc(S["min_done"], 1)

            def soft_centre(c, p, n):
                lv = logit[:, :].rearrange("p (h m) -> p h m", h=H)
                dve.wait_ge(S["min_done"], c + 1)
                if n >= 1:
                    dve.wait_ge(S["prob_done"], c)
                nc.vector.tensor_tensor(logit_c[:, :].rearrange("p (h m) -> p h m", h=H), lv,
                                        logit_min[:, :].unsqueeze(2).broadcast_to([P, H, M]), ALU.subtract).then_inc(S["centred"], 1)

            def prob_scale(c, p, n):
                dve.wait_ge(S["prob_done"], c + 1)
                if n >= 1:
                    dve.wait_ge(S["pz_turned"], c)
                nc.vector.tensor_tensor(pz[:, :], prob[:, :], slot_inv[:, p, HM:2 * HM], ALU.mult).then_inc(S["pz_done"], 1)

            def prob_total(c, p, n):
                dve.wait_ge(S["prob_done"], c + 1)
                nc.vector.reduce_sum(prob_sum[:, :], prob[:, :].rearrange("p (h m) -> p h m", h=H), AX_X).then_inc(S["prob_summed"], 1)

            def prob_invert(c, p, n):
                dve.wait_ge(S["prob_summed"], c + 1)
                if n >= 2:
                    dve.wait_ge(S["o1_done"], c - 1)
                nc.vector.reciprocal(prob_inv[:, p, :], prob_sum[:, :]).then_inc(S["pinv_done"], 1)

            def mask_a(c, p, n):
                dve.wait_ge(S["a_done"], c + 1)
                if n >= 1:
                    dve.wait_ge(S["o_done"], c)
                nc.vector.tensor_tensor(a_masked[:, :, :], c_ps[:, :].rearrange("p (h t) -> p h t", h=H),
                                        tri.unsqueeze(1).broadcast_to([P, H, P]), ALU.mult).then_inc(S["a_mask_done"], 1)

            def early_moments(c, p, n):
                if n == NC - 1:
                    for g in range(NG - 1):
                        moments(2, g)

            def norm_shares(c, p, n):
                dve.wait_ge(S["o_done"], c + 1)
                dve.wait_ge(S["pinv_done"], c + 1)
                if n >= 1:
                    dve.wait_ge(S["o2_done"], c)
                    dve.wait_ge(S["sq_done"], c)
                nc.vector.tensor_tensor(o1[:, :].rearrange("p (h d) -> p h d", h=H), o_ps.rearrange("p (h d) -> p h d", h=H),
                                        prob_inv[:, p, :].unsqueeze(2).broadcast_to([P, H, DK]), ALU.mult).then_inc(S["o1_done"], 1)

            def norm_squares(c, p, n):
                dve.wait_ge(S["sq_done"], c + 1)
                nc.vector.reduce_sum(o_ss[:, :], o_sq[:, :].rearrange("p (h d) -> p h d", h=H), AX_X).then_inc(S["ss_done"], 1)

            def norm_variance(c, p, n):
                dve.wait_ge(S["ss_done"], c + 1)
                if n >= 1:
                    dve.wait_ge(S["orstd_done"], c)
                nc.vector.tensor_scalar(o_var[:, :], o_ss[:, :], DK * EPS, None, ALU.add).then_inc(S["o_var_done"], 1)

            def norm_apply(c, p, n):
                dve.wait_ge(S["orstd_done"], c + 1)
                dve.wait_ge(S["o2_done"], c + 1)
                if n >= 1:
                    dve.wait_ge(S["o_turned"], c)
                nc.vector.scalar_tensor_tensor(o3[:, :].rearrange("p (h d) -> p h d", h=H), o2[:, :].rearrange("p (h d) -> p h d", h=H),
                                               DK ** 0.5, o_rstd[:, :].unsqueeze(2).broadcast_to([P, H, DK]), ALU.mult,
                                               ALU.mult).then_inc(S["o3_done"], 1)

            def add_y(c, p, n):
                dve.wait_ge(S["y_done"], c + 1)
                nc.vector.tensor_tensor(x[:, c, :], y_ps, x[:, c, :], ALU.add).then_inc(S["y_added"], 1)

            def attn_step(i, n):
                front, mid, last, end = stages(i, n)
                if front:
                    rope_multiply(*front)
                if end:
                    norm_apply(*end)
                if front:
                    clip_slots(*front)
                if last:
                    mask_a(*last)
                if last:
                    early_moments(*last)
                if mid:
                    sums_product(*mid)
                if mid:
                    sums_inverse(*mid)
                if end:
                    add_y(*end)
                if mid:
                    soft_scale(*mid)
                if mid:
                    soft_min(*mid)
                if last:
                    norm_shares(*last)
                if mid:
                    soft_centre(*mid)
                if front:
                    spread_q(*front)
                if mid:
                    prob_scale(*mid)
                if last:
                    norm_squares(*last)
                if mid:
                    prob_total(*mid)
                if last:
                    norm_variance(*last)
                if mid:
                    prob_invert(*mid)
                if front:
                    mask_s(*front)

            def before(i):
                if i == NC + 2:
                    centre(2, 0)
                    centre(2, 1)

            moments(0, 0)
            centre(0, 0)
            moments(0, 1)
            centre(0, 1)
            moments(0, 2)
            moments(0, 3)
            centre(0, 2)
            low_part(0, 0)
            split_first()
            centre(0, 3)
            low_part(0, 1)
            low_part(0, 2)
            low_part(0, 3)
            route_z(0)
            ffn(0)
            low_part(1, 0)
            centre(1, 3)
            low_part(1, 1)
            low_part(1, 2)
            prepare(0)
            low_part(1, 3)
            for g in range(1, NG):
                prepare(g)
            attention(dve, attn_step, before)
            moments(2, 3)
            centre(2, 2)
            low_part(2, 0)
            centre(2, 3)
            low_part(2, 1)
            low_part(2, 2)
            low_part(2, 3)
            route_z(1)
            ffn(1)

        @block.tensor
        def _(pe):
            mm = nc.tensor.matmul

            def turn(k, g):
                n = NG * k + g
                pe.wait_ge(xn_done, n + 1)
                pe.wait_ge(xn_last_done, n + 1)
                if k == 2 and g == 0:
                    pe.wait_ge(S["q_t_copied"], NC)
                    pe.wait_ge(S["clip_done"], NC)
                elif g >= 2:
                    pe.wait_ge(xt_lo_done, n - 1)
                for c in range(GT):
                    i = nc.tensor.transpose(xt_ps[k][g % 2][:, c * P:(c + 1) * P], xn[:, g % 2, c, :], ident)
                i.then_inc(xt_turned, 1)

            def router(f, g):
                pe.wait_ge(wr_split, 1)
                if f and g == 0:
                    pe.wait_ge(S["o1_done"], NC)
                pe.wait_ge(xt_lo_done, NG * 2 * f + g + 1)
                for c in range(g * GT, (g + 1) * GT):
                    ts = slice(c * P, (c + 1) * P)
                    dst = router_ps[:, c * ER:(c + 1) * ER]
                    mm(dst, xt_hi[:, ts], wr_hi[:, :], start=True, stop=False)
                    mm(dst, xt_hi[:, ts], wr_lo[:, :], start=False, stop=False)
                    i = mm(dst, xt_lo[:, ts], wr_hi[:, :], start=False, stop=True)
                i.then_inc(router_done, 1)

            def wcols(parts, e, at, n):
                return parts[:, e, at:at + n]

            def down_half(f, e, g, j):
                s = SPF * f + NG * e + g
                pe.wait_ge(hlo_done, 2 * s + 2)
                if not (f == 0 and isinstance(e, int) and e == 0 and g == 0):
                    pe.wait_ge(added, 2 * (s - 1) + j + 1)
                if isinstance(e, int) and e == 0 and g == 0 and j == 1:
                    pe.wait_ge(z_done, f + 1)
                for c in range(2 * j, 2 * j + 2):
                    dst = down_ps[j][:, c % 2 * P:(c % 2 + 1) * P]
                    k = 0
                    for ih in range(IH):
                        at = 2 * I + ih * D
                        for hp, wp in ((h_hi, w_hi), (h_hi, w_lo), (h_lo, w_hi)):
                            i = mm(dst, hp[:, g, ih, c * P:(c + 1) * P], wcols(wp, e, at, D),
                                   start=(k == 0), stop=(k == 3 * IH - 1))
                            k += 1
                i.then_inc(down_done, 1)

            def unit(f, e, g, ih, first):
                u = IH * (SPF * f + NG * e + g) + ih
                if not (f == 0 and first):
                    pe.wait_ge(hmul_done, u - 1)
                ts = slice(g * GW, (g + 1) * GW)
                for at, ps, done in ((ih * P, gate_ps[ih], gate_done), (I + ih * P, up_ps[ih], up_done)):
                    mm(ps[:, :], wcols(w_hi, e, at, P), xt_hi[:, ts], start=True, stop=False)
                    mm(ps[:, :], wcols(w_lo, e, at, P), xt_hi[:, ts], start=False, stop=False)
                    mm(ps[:, :], wcols(w_hi, e, at, P), xt_lo[:, ts], start=False, stop=True).then_inc(done, 1)

            def ffn(f):
                pe.wait_ge(wlo0_done, 1)
                if f:
                    pe.wait_ge(S["y_added"], NC)
                for g in range(NG):
                    unit(f, 0, g, 0, g == 0)
                    if g >= 2:
                        down_half(f, 0, g - 2, 1)
                    unit(f, 0, g, 1, g == 0)
                    if g >= 1:
                        down_half(f, 0, g - 1, 0)
                with pe.Fori(1, E - 1 if f == 0 else E) as e:
                    if f == 0:
                        pe.wait_ge(wlo_done, e)
                    step(f, e, e - 1)
                if f == 0:
                    pe.wait_ge(wlo_done, E - 1)
                    step(f, E - 1, E - 2)
                down_half(f, E - 1, NG - 2, 1)
                for j in range(2):
                    down_half(f, E - 1, NG - 1, j)

            def step(f, e, before):
                for g in range(NG):
                    unit(f, e, g, 0, False)
                    down_half(f, e if g >= 2 else before, (g - 2) % NG, 1)
                    unit(f, e, g, 1, False)
                    down_half(f, e if g >= 1 else before, (g - 1) % NG, 0)

            def three(dst, a, b, signal):
                mm(dst, a[0], b[0], start=True, stop=False)
                mm(dst, a[0], b[1], start=False, stop=False)
                mm(dst, a[1], b[0], start=False, stop=True).then_inc(signal, 1)

            def prepare(g):
                ts = slice(g * GW, (g + 1) * GW)
                pe.wait_ge(xt_lo_done, NG + g + 1)
                if g == 0:
                    pe.wait_ge(wlo_done, E + 1)
                    pe.wait_ge(added, 2 * SPF)
                if g >= 2:
                    pe.wait_ge(S["low_lo_done"], g - 1)
                three(low_ps[g % 2], (wlow_hi[:, :], wlow_lo[:, :]), (xt_hi[:, ts], xt_lo[:, ts]), S["low_turned"])
                for ps, at, done, read in ((v_ps[g % 2], 2 * D, "v_projected", "v_copied"), (g_ps[g % 2], 3 * D, "g_projected", "gate_silu")):
                    if g >= 2:
                        pe.wait_ge(S[read], g - 1)
                    for c in range(GT):
                        ts = slice((g * GT + c) * P, (g * GT + c + 1) * P)
                        dst, ws = ps[:, c * D:(c + 1) * D], slice(at, at + D)
                        mm(dst, xt_hi[:, ts], wqkvg_hi[:, ws], start=True, stop=False)
                        mm(dst, xt_hi[:, ts], wqkvg_lo[:, ws], start=False, stop=False)
                        i = mm(dst, xt_lo[:, ts], wqkvg_hi[:, ws], start=False, stop=True)
                    i.then_inc(S[done], 1)

            def project(c, p, n):
                if n >= 1:
                    pe.wait_ge(S["q_t_copied"], c)
                else:
                    pe.wait_ge(S["v_copied"], NG)
                three(qk_ps[:, 0:2 * D], (xt_hi[:, bass.ds(c * P, P)], xt_lo[:, bass.ds(c * P, P)]),
                      (wqkvg_hi[:, 0:2 * D], wqkvg_lo[:, 0:2 * D]), S["projected"])

            def slot_logits(c, p, n):
                if n >= 1:
                    pe.wait_ge(S["clip_done"], c)
                else:
                    pe.wait_ge(wlo_done, E + 2)
                    pe.wait_ge(S["low_lo_done"], NG)
                three(slots_ps[:, :], (low_hi[:, bass.ds(c * P, P)], low_lo[:, bass.ds(c * P, P)]),
                      (wslots_hi[:, :], wslots_lo[:, :]), S["slots_done"])

            def turn_qk(c, p, n):
                pe.wait_ge(S["qk_lo_done"], c + 1)
                nc.tensor.transpose(q_t_ps, qk[:, p, 0:D], ident)
                for a, part in enumerate((qk_hi[:, 0:D], qk_lo[:, 0:D], qk_hi[:, D:2 * D], qk_lo[:, D:2 * D])):
                    i = nc.tensor.transpose(qk_t_ps[:, a * P:(a + 1) * P], part, ident16[:, :])
                i.then_inc(S["qk_turned"], 1)

            def scores(c, p, n):
                pe.wait_ge(S["q_spread"], c + 1)
                if n >= 1:
                    pe.wait_ge(S["logit_scaled"], c)
                else:
                    pe.wait_ge(S["gate_silu"], NG)
                three(s_ps[:, :], (qk_t[:, p, 2, :], qk_t[:, p, 3, :]), (q_heads[:, p, 0, :, :], q_heads[:, p, 1, :, :]), S["s_done"])

            def turn_v(c, p, n):
                pe.wait_ge(S["slots_exp"], c + 1)
                if n >= 1:
                    pe.wait_ge(S["p_copied"], c)
                for a in range(2):
                    i = nc.tensor.transpose(vslot_t_ps[:, a * P:(a + 1) * P], slots[:, p, HM + a * P:HM + (a + 1) * P], ident)
                i.then_inc(S["vslot_turned"], 1)

            def running_sums(c, p, n):
                pe.wait_ge(S["slots_b3"], c + 1)
                if n == 0:
                    pe.wait_ge(S["low_lo_done"], NG)
                for k, part in enumerate((slot_b1, slot_b2, slot_b3)):
                    i = mm(sum_ps[:, :], tri16[:, :], part[:, p, :], start=(n == 0 and k == 0), stop=True, skip_group_check=True)
                i.then_inc(S["sums_done"], 1)

            def logits_of_earlier(c, p, n):
                pe.wait_ge(S["s_mask_done"], c + 1)
                if n >= 1:
                    pe.wait_ge(S["state_copied"], c)
                    pe.wait_ge(S["q_t_copied"], c + 1)
                    mm(logit_ps, q_t[:, p, :], state[:, p, 0:HM], start=True, stop=False, skip_group_check=True)

            def logits_of_chunk(c, p, n):
                pe.wait_ge(S["s_mask_done"], c + 1)
                for h in range(H):
                    hs = slice(h * M, (h + 1) * M)
                    i = mm(logit_ps[:, hs], s_masked[:, p, h, :], slots[:, p, hs], start=(n == 0), stop=True, skip_group_check=True)
                i.then_inc(S["logits_done"], 1)

            def add_sums(c, p, n):
                pe.wait_ge(S["sums_prod"], c + 1)
                for part in (slot_b1, slot_b2, slot_b3):
                    mm(sum_ps[:, :], rest16[:, :], part[:, p, :], start=False, stop=True, skip_group_check=True)

            def add_state(c, p, n):
                if n >= 1:
                    pe.wait_ge(S["state_copied"], c)
                mm(state_ps[:, 0:HM], qk[:, p, D:2 * D], slots[:, p, 0:HM], start=False, stop=True, skip_group_check=True)
                for a in range(2):
                    i = mm(state_ps[:, HM + a * 2 * DK:HM + (a + 1) * 2 * DK], slots[:, p, HM + a * P:HM + (a + 1) * P],
                           v_all[:, c, a * 2 * DK:(a + 1) * 2 * DK], start=False, stop=True, skip_group_check=True)
                i.then_inc(S["back_done"], 1)

            def turn_p(c, p, n):
                pe.wait_ge(S["pz_done"], c + 1)
                pe.wait_ge(S["vslot_copied"], c + 1)
                for a in range(2):
                    i = nc.tensor.transpose(pz_t_ps[:, a * P:(a + 1) * P], pz[:, a * P:(a + 1) * P], ident)
                i.then_inc(S["pz_turned"], 1)

            def weights_a(c, p, n):
                pe.wait_ge(S["p_copied"], c + 1)
                pe.wait_ge(S["vslot_copied"], c + 1)
                if n >= 1:
                    pe.wait_ge(S["o1_done"], c)
                for j, done in enumerate(("a_even", "a_done")):
                    rows = slice(j * M, (j + 1) * M)
                    for a in range(2):
                        i = mm(c_ps[:, (2 * a + j) * P:(2 * a + j + 1) * P], vslot_t[rows, p, a, :], p_t[rows, p, a, :], start=True, stop=True)
                    i.then_inc(S[done], 1)
                    if j == 0:
                        pe.wait_ge(S["a_even"], c + 1)

            def outputs(c, p, n):
                pe.wait_ge(S["a_mask_done"], c + 1)
                for h in range(H):
                    hs = slice(h * DK, (h + 1) * DK)
                    if n >= 1 and h % 2 == 0:
                        pair = slice(h * DK, (h + 2) * DK)
                        mm(o_ps[:, pair], p_t[:, p, h // 2, :], state[:, p, HM + h * DK:HM + (h + 2) * DK],
                           start=True, stop=True, skip_group_check=True)
                    i = mm(o_ps[:, hs], a_masked[:, h, :], v_all[:, c, hs], start=(n == 0), stop=True, skip_group_check=True)
                i.then_inc(S["o_done"], 1)

            def turn_o(c, p, n):
                pe.wait_ge(S["o3_done"], c + 1)
                if n >= 1:
                    pe.wait_ge(S["y_added"], c)
                nc.tensor.transpose(o_t_ps, o3[:, :], ident).then_inc(S["o_turned"], 1)

            def out_proj(c, p, n):
                pe.wait_ge(S["o_copied"], c + 1)
                mm(y_ps, o_t[:, :], wo[:, :], start=True, stop=True).then_inc(S["y_done"], 1)

            def attn_step(i, n):
                front, mid, last, end = stages(i, n)
                if front:
                    project(*front)
                if mid:
                    running_sums(*mid)
                if mid:
                    turn_v(*mid)
                if front:
                    slot_logits(*front)
                if end:
                    turn_o(*end)
                if last:
                    weights_a(*last)
                if mid:
                    logits_of_earlier(*mid)
                if end:
                    out_proj(*end)
                if mid:
                    logits_of_chunk(*mid)
                if front:
                    turn_qk(*front)
                if last:
                    outputs(*last)
                if mid:
                    add_state(*mid)
                if mid:
                    add_sums(*mid)
                if front:
                    scores(*front)
                if mid:
                    turn_p(*mid)

            pe.wait_ge(consts_loaded, 16)
            turn(0, 0)
            turn(0, 1)
            router(0, 0)
            turn(0, 2)
            router(0, 1)
            turn(0, 3)
            router(0, 2)
            router(0, 3)
            ffn(0)
            for g in range(NG - 1):
                turn(1, g)
            prepare(0)
            turn(1, 3)
            for g in range(1, NG):
                prepare(g)
            pe.wait_ge(S["low_lo_done"], NG)
            mm(state_ps[:, 0:HM + 4 * DK], zero16[:, 0:P], zero16[:, :], start=True, stop=True, skip_group_check=True)
            attention(pe, attn_step)
            turn(2, 0)
            turn(2, 1)
            router(1, 0)
            turn(2, 2)
            router(1, 1)
            turn(2, 3)
            router(1, 2)
            router(1, 3)
            ffn(1)


def stages(i, n):
    return [(i - late, (n - late) % 2, n - late) if 0 <= n - late < NC else None
            for late in range(4)]


def attention(eng, step, before=None):
    for i in range(4):
        step(i, i)
    with eng.Fori(2, NC // 2) as k:
        step(2 * k, 4)
        step(2 * k + 1, 5)
    for i in range(NC, NC + 3):
        if before:
            before(i)
        step(i, i)


def kernel(**inputs):
    import numpy as _np
    import concourse.bacc as _bacc
    from concourse import mybir as _mybir
    from concourse.bass_utils import run_bass_kernel_spmd as _run

    a = {k.replace("L0_", ""): _np.asarray(v) for k, v in inputs.items()}
    gate = _np.concatenate([a["ffn_shared_gate"].T[None], a["ffn_gate_w"]])
    up = _np.concatenate([a["ffn_shared_up"].T[None], a["ffn_up_w"]])
    down = _np.concatenate([a["ffn_shared_down"].T[None], a["ffn_down_w"]])
    down = down.reshape(E, IH, P, D).transpose(0, 2, 1, 3).reshape(E, P, IH * D)
    slots = _np.zeros((P, 2 * HM), _np.float32)
    slots[0:LOW, 0:HM] = a["attn_sk_w2"]
    slots[LOW:2 * LOW, HM:] = a["attn_sv_w2"]
    slots[2 * LOW, 0:HM] = a["attn_sk_b2"]
    slots[2 * LOW, HM:] = a["attn_sv_b2"]
    arrays = {
        "x": a["attn_hidden_states"].reshape(T, D),
        "consts": constants(),
        "w_ffn": _np.concatenate([gate, up, down], axis=2),
        "w_router": a["ffn_router_w"].T,
        "router_bias": _np.broadcast_to(a["ffn_routing_bias"], (P, ER)),
        "w_qkvg": _np.concatenate([a["attn_Wq"], a["attn_Wk"], a["attn_Wv"], a["attn_Wg"]], axis=1),
        "w_low": _np.concatenate([a["attn_sk_w1"], a["attn_sv_w1"]], axis=1),
        "w_slots": slots,
        "w_out": a["attn_Wo"],
        "gnorm": _np.broadcast_to(_np.tile(a["attn_gnorm_w"], H), (P, D)),
    }
    nc = _bacc.Bacc("TRN2", target_bir_lowering=False, num_devices=1)
    arrays = {f"in_{k}": _np.ascontiguousarray(v) for k, v in arrays.items()}
    args = [nc.dram_tensor(k, v.shape, _mybir.dt.from_np(v.dtype), kind="ExternalInput").ap() for k, v in arrays.items()]
    args.append(nc.dram_tensor("out_dram", (T, D), _mybir.dt.float32, kind="ExternalOutput").ap())
    macaron_kernel(nc, *args)
    r = _run(nc, [arrays], core_ids=[0])
    return r.results[0]["out_dram"].reshape(1, T, D)
```
